# Optimizing a Trainium2 kernel written in Bass

```python
import numpy as np
import jax
import jax.numpy as jnp

def _softmax(x, axis=-1):
    return jax.nn.softmax(x, axis=axis)

def _gelu(x):
    return jax.nn.gelu(x, approximate=True)

def _silu(x):
    return jax.nn.silu(x)

def _sigmoid(x):
    return jax.nn.sigmoid(x)

def _layernorm(x, axis=-1, eps=1e-05):
    m = jnp.mean(x, axis=axis, keepdims=True)
    v = jnp.var(x, axis=axis, keepdims=True)
    return (x - m) / jnp.sqrt(v + eps)

def _scatter_add(tgt, idx, src, axis=0):
    return tgt.at[idx].add(src)

def _segment_sum(src, seg, n):
    return jax.ops.segment_sum(src, seg, n)
kernel_name = 'mk_gps_d2_gnn_r32_218cba'

def setup_inputs(seed: int=0):
    np.random.seed(seed)
    _w = jnp.asarray

    def _rec_inputs():
        import jax
        import jax.numpy as jnp
        _gk = jax.random.key(seed)
        x = -8.776e-05 + 1 * jax.random.normal(jax.random.fold_in(_gk, 1), (3125, 256), jnp.float32)
        src = jax.random.randint(jax.random.fold_in(_gk, 2), (50000,), 0, 3125, jnp.int32)
        dst = jnp.minimum((3125 * jax.random.uniform(jax.random.fold_in(_gk, 3), (50000,)) ** 2.0).astype(jnp.int32), 99999)
        _o = jnp.argsort(dst, stable=True)
        src = src[_o]
        dst = dst[_o]
        edge_attr_128 = -0.000128692 + 0.999872 * jax.random.normal(jax.random.fold_in(_gk, 11), (50000, 128), jnp.float32)
        return (x, src, dst, edge_attr_128)
    x, src, dst, edge_attr_128 = _rec_inputs()

    def _L0_gnn_setup():
        import jax, jax.numpy as jnp
        import numpy as np
        N_NODES = 625
        N_EDGES = 10000
        D_IN_N, D_OUT_N = (256, 256)
        D_IN_E, D_OUT_E = (128, 128)
        D_MODEL = 256
        N_HEADS = 2

        def segment_softmax(scores, seg, num_segments):
            m = jax.ops.segment_max(scores, seg, num_segments=num_segments)
            e = jnp.exp(scores - m[seg])
            den = jax.ops.segment_sum(e, seg, num_segments=num_segments)
            return e / den[seg]
        key = jax.random.key(seed)
        ks = jax.random.split(key, 16)
        s = 0.05
        return {'node_features': jax.random.normal(ks[0], (N_NODES, D_IN_N), jnp.float32), 'edge_features': jax.random.normal(ks[1], (N_EDGES, D_IN_E), jnp.float32), 'edge_index': jax.random.randint(ks[2], (2, N_EDGES), 0, N_NODES, jnp.int32), 'W1w': jax.random.normal(ks[3], (N_HEADS, D_OUT_N, D_IN_N), jnp.float32) * s, 'W1b': jax.random.normal(ks[4], (N_HEADS, D_OUT_N), jnp.float32) * s, 'W2w': jax.random.normal(ks[5], (N_HEADS, D_OUT_E, D_IN_E), jnp.float32) * s, 'W2b': jax.random.normal(ks[6], (N_HEADS, D_OUT_E), jnp.float32) * s, 'W3w': jax.random.normal(ks[7], (N_HEADS, D_MODEL, D_OUT_N + D_OUT_E + D_IN_N), jnp.float32) * s, 'W3b': jax.random.normal(ks[8], (N_HEADS, D_MODEL), jnp.float32) * s, 'aVw': jax.random.normal(ks[9], (N_HEADS, 1, 2 * D_OUT_N), jnp.float32) * s, 'aVb': jax.random.normal(ks[10], (N_HEADS, 1), jnp.float32) * s, 'aEw': jax.random.normal(ks[11], (N_HEADS, 1, 2 * D_OUT_N + D_OUT_E), jnp.float32) * s, 'aEb': jax.random.normal(ks[12], (N_HEADS, 1), jnp.float32) * s}
    _L0_gnn_all = _L0_gnn_setup()
    _L0_gnn_in = {k: v for k, v in _L0_gnn_all.items() if k in ('W1w', 'W1b', 'W2w', 'W2b', 'W3w', 'W3b', 'aVw', 'aVb', 'aEw', 'aEb')}
    del _L0_gnn_all

    def _L0_mix_setup():
        import jax, jax.numpy as jnp
        import numpy as np
        HEADS = 4
        DIM_HEAD = 32
        key = jax.random.key(seed)
        k1, k2, k3 = jax.random.split(key, 3)
        B, L, D = (16, 256, 256)
        hidden = HEADS * DIM_HEAD
        x = jax.random.normal(k1, (B, L, D), dtype=jnp.float32)
        W_qkv = jax.random.normal(k2, (D, 3 * hidden), dtype=jnp.float32) * D ** (-0.5)
        W_out = jax.random.normal(k3, (hidden, D), dtype=jnp.float32) * hidden ** (-0.5)
        b_out = jnp.zeros((D,), dtype=jnp.float32)
        return {'x': x, 'W_qkv': W_qkv, 'W_out': W_out, 'b_out': b_out}
    _L0_mix_all = _L0_mix_setup()
    _L0_mix_in = {k: v for k, v in _L0_mix_all.items() if k in ('W_qkv', 'W_out', 'b_out')}
    del _L0_mix_all

    def _L0_ffn_setup():
        import math
        import jax, jax.numpy as jnp
        import numpy as np
        CAPACITY_FACTOR = 1.25
        TOP_K = 2
        LN_EPS = 1e-05

        def _layer_norm(x, gamma, beta):
            mu = jnp.mean(x, axis=-1, keepdims=True)
            var = jnp.var(x, axis=-1, keepdims=True)
            return (x - mu) * jax.lax.rsqrt(var + LN_EPS) * gamma + beta
        key = jax.random.key(seed)
        ks = jax.random.split(key, 4)
        B, S, D, F, E = (8, 128, 256, 512, 8)
        x = jax.random.normal(ks[0], (B, S, D), dtype=jnp.float32)
        Wr = jax.random.normal(ks[1], (D, E), dtype=jnp.float32) / np.sqrt(D)
        br = jnp.zeros((E,), jnp.float32)
        W1 = jax.random.normal(ks[2], (E, D, F), dtype=jnp.float32) / np.sqrt(D)
        b1 = jnp.zeros((E, F), jnp.float32)
        W2 = jax.random.normal(ks[3], (E, F, D), dtype=jnp.float32) / np.sqrt(F)
        b2 = jnp.zeros((E, D), jnp.float32)
        gamma = jnp.ones((D,), jnp.float32)
        beta = jnp.zeros((D,), jnp.float32)
        return {'x': x, 'Wr': Wr, 'br': br, 'W1': W1, 'b1': b1, 'W2': W2, 'b2': b2, 'gamma': gamma, 'beta': beta}
    _L0_ffn_all = _L0_ffn_setup()
    _L0_ffn_in = {k: v for k, v in _L0_ffn_all.items() if k in ('Wr', 'br', 'W1', 'b1', 'W2', 'b2', 'gamma', 'beta')}
    del _L0_ffn_all

    def _L1_gnn_setup():
        import jax, jax.numpy as jnp
        import numpy as np
        ALPHA = 0.2
        N_NODES = 3125
        N_EDGES = 50000
        NFEAT = 256
        HID = 64
        NHEADS = 4

        def _gat_head(x, src, dst, Wh, ah, n_nodes):
            hid = Wh.shape[1]
            h = x @ Wh
            h = jnp.where(jnp.isnan(h), 0.0, h)
            a1, a2 = (ah[0, :hid], ah[0, hid:])
            alpha_src = h @ a1
            alpha_dst = h @ a2
            s = alpha_src[src] + alpha_dst[dst]
            e = jnp.exp(-jax.nn.leaky_relu(s, ALPHA))
            e = jnp.where(jnp.isnan(e), 0.0, e)
            rowsum = jax.ops.segment_sum(e, src, num_segments=n_nodes)
            hp = jax.ops.segment_sum(e[:, None] * h[dst], src, num_segments=n_nodes)
            hp = jnp.where(jnp.isnan(hp), 0.0, hp)
            hp = hp / rowsum[:, None]
            hp = jnp.where(jnp.isnan(hp), 0.0, hp)
            return jax.nn.elu(hp)
        key = jax.random.key(seed)
        k1, k2, k3, k4 = jax.random.split(key, 4)
        x = jax.random.normal(k1, (N_NODES, NFEAT), dtype=jnp.float32)
        edge_index = jax.random.randint(k2, (2, N_EDGES), 0, N_NODES, dtype=jnp.int64)
        W = jax.random.normal(k3, (NHEADS, NFEAT, HID), dtype=jnp.float32) * (1.414 * np.sqrt(2.0 / (NFEAT + HID)))
        a = jax.random.normal(k4, (NHEADS, 1, 2 * HID), dtype=jnp.float32) * (1.414 * np.sqrt(2.0 / (1 + 2 * HID)))
        return {'x': x, 'edge_index': edge_index, 'W': W, 'a': a}
    _L1_gnn_all = _L1_gnn_setup()
    _L1_gnn_in = {k: v for k, v in _L1_gnn_all.items() if k in ('W', 'a')}
    del _L1_gnn_all

    def _L1_mix_setup():
        import jax, jax.numpy as jnp
        import numpy as np
        B, N, C, H = (8, 512, 256, 8)
        D = C // H
        GH = C // 4
        key = jax.random.key(seed)
        ks = jax.random.split(key, 6)
        s = 0.02
        return {'x': jax.random.normal(ks[0], (B, N, C), dtype=jnp.float32), 'Wqkv': jax.random.normal(ks[1], (C, 3 * C), dtype=jnp.float32) * s, 'Wproj': jax.random.normal(ks[2], (C, C), dtype=jnp.float32) * s, 'bproj': jnp.zeros((C,), dtype=jnp.float32), 'ln_g': jnp.ones((C,), dtype=jnp.float32), 'ln_b': jnp.zeros((C,), dtype=jnp.float32), 'Wg1': jax.random.normal(ks[3], (C, GH), dtype=jnp.float32) * s, 'bg1': jnp.zeros((GH,), dtype=jnp.float32), 'Wg2': jax.random.normal(ks[4], (GH, C), dtype=jnp.float32) * s, 'bg2': jnp.zeros((C,), dtype=jnp.float32)}
    _L1_mix_all = _L1_mix_setup()
    _L1_mix_in = {k: v for k, v in _L1_mix_all.items() if k in ('Wqkv', 'Wproj', 'bproj', 'ln_g', 'ln_b', 'Wg1', 'bg1', 'Wg2', 'bg2')}
    del _L1_mix_all

    def _L1_ffn_setup():
        import math
        import jax, jax.numpy as jnp
        import numpy as np
        CAPACITY_FACTOR = 1.25
        key = jax.random.key(seed)
        ks = jax.random.split(key, 5)
        B, L, D, F, E = (8, 256, 256, 1024, 8)
        h = jax.random.normal(ks[0], (B, L, D), dtype=jnp.float32)
        gate_w = jax.random.normal(ks[1], (D, E), dtype=jnp.float32) * 0.02
        gate_b = jnp.zeros((E,), dtype=jnp.float32)
        w1 = jax.random.normal(ks[2], (E, D, F), dtype=jnp.float32) * (1.0 / math.sqrt(D))
        b1 = jnp.zeros((E, F), dtype=jnp.float32)
        w2 = jax.random.normal(ks[3], (E, F, D), dtype=jnp.float32) * (1.0 / math.sqrt(F))
        b2 = jnp.zeros((E, D), dtype=jnp.float32)
        return {'h': h, 'gate_w': gate_w, 'gate_b': gate_b, 'w1': w1, 'b1': b1, 'w2': w2, 'b2': b2}
    _L1_ffn_all = _L1_ffn_setup()
    _L1_ffn_in = {k: v for k, v in _L1_ffn_all.items() if k in ('gate_w', 'gate_b', 'w1', 'b1', 'w2', 'b2')}
    del _L1_ffn_all
    return {'x': x, 'src': src, 'dst': dst, 'edge_attr_128': edge_attr_128, 'L0_gnn_W1w': _L0_gnn_in['W1w'], 'L0_gnn_W1b': _L0_gnn_in['W1b'], 'L0_gnn_W2w': _L0_gnn_in['W2w'], 'L0_gnn_W2b': _L0_gnn_in['W2b'], 'L0_gnn_W3w': _L0_gnn_in['W3w'], 'L0_gnn_W3b': _L0_gnn_in['W3b'], 'L0_gnn_aVw': _L0_gnn_in['aVw'], 'L0_gnn_aVb': _L0_gnn_in['aVb'], 'L0_gnn_aEw': _L0_gnn_in['aEw'], 'L0_gnn_aEb': _L0_gnn_in['aEb'], 'L0_mix_W_qkv': _L0_mix_in['W_qkv'], 'L0_mix_W_out': _L0_mix_in['W_out'], 'L0_mix_b_out': _L0_mix_in['b_out'], 'L0_ffn_Wr': _L0_ffn_in['Wr'], 'L0_ffn_br': _L0_ffn_in['br'], 'L0_ffn_W1': _L0_ffn_in['W1'], 'L0_ffn_b1': _L0_ffn_in['b1'], 'L0_ffn_W2': _L0_ffn_in['W2'], 'L0_ffn_b2': _L0_ffn_in['b2'], 'L0_ffn_gamma': _L0_ffn_in['gamma'], 'L0_ffn_beta': _L0_ffn_in['beta'], 'L1_gnn_W': _L1_gnn_in['W'], 'L1_gnn_a': _L1_gnn_in['a'], 'L1_mix_Wqkv': _L1_mix_in['Wqkv'], 'L1_mix_Wproj': _L1_mix_in['Wproj'], 'L1_mix_bproj': _L1_mix_in['bproj'], 'L1_mix_ln_g': _L1_mix_in['ln_g'], 'L1_mix_ln_b': _L1_mix_in['ln_b'], 'L1_mix_Wg1': _L1_mix_in['Wg1'], 'L1_mix_bg1': _L1_mix_in['bg1'], 'L1_mix_Wg2': _L1_mix_in['Wg2'], 'L1_mix_bg2': _L1_mix_in['bg2'], 'L1_ffn_gate_w': _L1_ffn_in['gate_w'], 'L1_ffn_gate_b': _L1_ffn_in['gate_b'], 'L1_ffn_w1': _L1_ffn_in['w1'], 'L1_ffn_b1': _L1_ffn_in['b1'], 'L1_ffn_w2': _L1_ffn_in['w2'], 'L1_ffn_b2': _L1_ffn_in['b2']}

def reference(x, src, dst, edge_attr_128, L0_gnn_W1w, L0_gnn_W1b, L0_gnn_W2w, L0_gnn_W2b, L0_gnn_W3w, L0_gnn_W3b, L0_gnn_aVw, L0_gnn_aVb, L0_gnn_aEw, L0_gnn_aEb, L0_mix_W_qkv, L0_mix_W_out, L0_mix_b_out, L0_ffn_Wr, L0_ffn_br, L0_ffn_W1, L0_ffn_b1, L0_ffn_W2, L0_ffn_b2, L0_ffn_gamma, L0_ffn_beta, L1_gnn_W, L1_gnn_a, L1_mix_Wqkv, L1_mix_Wproj, L1_mix_bproj, L1_mix_ln_g, L1_mix_ln_b, L1_mix_Wg1, L1_mix_bg1, L1_mix_Wg2, L1_mix_bg2, L1_ffn_gate_w, L1_ffn_gate_b, L1_ffn_w1, L1_ffn_b1, L1_ffn_w2, L1_ffn_b2):
    import jax
    import jax.numpy as jnp

    def _L0_gnn_ref(node_features, edge_features, edge_index, W1w, W1b, W2w, W2b, W3w, W3b, aVw, aVb, aEw, aEb):
        import jax, jax.numpy as jnp
        import numpy as np
        N_NODES = 625
        N_EDGES = 10000
        D_IN_N, D_OUT_N = (256, 256)
        D_IN_E, D_OUT_E = (128, 128)
        D_MODEL = 256
        N_HEADS = 2

        def segment_softmax(scores, seg, num_segments):
            m = jax.ops.segment_max(scores, seg, num_segments=num_segments)
            e = jnp.exp(scores - m[seg])
            den = jax.ops.segment_sum(e, seg, num_segments=num_segments)
            return e / den[seg]
        u, v = (edge_index[0], edge_index[1])
        N = node_features.shape[0]
        H = W1w.shape[0]
        dn = W1w.shape[1]
        de = W2w.shape[1]
        embs = []
        for i in range(H):
            h1 = node_features @ W1w[i].T + W1b[i]
            e2 = edge_features @ W2w[i].T + W2b[i]
            wVu, wVv = (aVw[i, 0, :dn], aVw[i, 0, dn:])
            sV = jax.nn.leaky_relu((h1 @ wVu)[u] + (h1 @ wVv)[v] + aVb[i, 0])
            aV = segment_softmax(sV, u, N)
            wEu, wEv, wEe = (aEw[i, 0, :dn], aEw[i, 0, dn:2 * dn], aEw[i, 0, 2 * dn:])
            sE = jax.nn.leaky_relu((h1 @ wEu)[u] + (h1 @ wEv)[v] + e2 @ wEe + aEb[i, 0])
            aE = segment_softmax(sE, u, N)
            m1 = aV[:, None] * node_features[v] @ W1w[i].T + W1b[i]
            m2 = aE[:, None] * edge_features @ W2w[i].T + W2b[i]
            W3a = W3w[i][:, :dn]
            W3bb = W3w[i][:, dn:dn + de]
            W3c = W3w[i][:, dn + de:]
            hc = node_features @ W3c.T
            msg = m1 @ W3a.T + m2 @ W3bb.T + hc[u] + W3b[i]
            embs.append(jax.ops.segment_sum(msg, u, num_segments=N))
        mean_emb = jnp.mean(jnp.stack(embs), axis=0)
        return jax.nn.softmax(mean_emb, axis=1)

    def _L0_mix_ref(x, W_qkv, W_out, b_out):
        import jax, jax.numpy as jnp
        import numpy as np
        HEADS = 4
        DIM_HEAD = 32
        B, L, D = x.shape
        scale = DIM_HEAD ** (-0.5)
        qkv = jnp.einsum('bld,df->blf', x, W_qkv)
        qkv = qkv.reshape(B, L, 3, HEADS, DIM_HEAD)
        q = jnp.transpose(qkv[:, :, 0], (0, 2, 1, 3)) * scale
        k = jax.nn.softmax(jnp.transpose(qkv[:, :, 1], (0, 2, 1, 3)), axis=2)
        v = jnp.transpose(qkv[:, :, 2], (0, 2, 1, 3))
        context = jnp.einsum('bhld,bhle->bhde', k, v)
        out = jnp.einsum('bhde,bhld->bhle', context, q)
        out = jnp.transpose(out, (0, 2, 1, 3)).reshape(B, L, HEADS * DIM_HEAD)
        return jnp.einsum('blf,fd->bld', out, W_out) + b_out

    def _L0_ffn_ref(x, Wr, br, W1, b1, W2, b2, gamma, beta):
        import math
        import jax, jax.numpy as jnp
        import numpy as np
        CAPACITY_FACTOR = 1.25
        TOP_K = 2
        LN_EPS = 1e-05

        def _layer_norm(x, gamma, beta):
            mu = jnp.mean(x, axis=-1, keepdims=True)
            var = jnp.var(x, axis=-1, keepdims=True)
            return (x - mu) * jax.lax.rsqrt(var + LN_EPS) * gamma + beta
        B, S, D = x.shape
        E = Wr.shape[1]
        N = B * S
        K = TOP_K
        logits = jnp.mean(x, axis=1) @ Wr + br
        routing_weights = jax.nn.softmax(logits, axis=-1)
        capacity = float(math.ceil(N * CAPACITY_FACTOR / E))
        expected_loads = routing_weights.sum(axis=0) * (N / B)
        scale = jnp.where(expected_loads > capacity, capacity / expected_loads, 1.0)
        routing_weights = jax.nn.softmax(routing_weights * scale, axis=-1)
        rw_tok = jnp.broadcast_to(routing_weights[:, None, :], (B, S, E)).reshape(N, E)
        top_w, top_i = jax.lax.top_k(rw_tok, K)
        top_w = jax.nn.softmax(top_w, axis=-1)
        xf = x.reshape(N, D)
        h = jax.nn.gelu(jnp.einsum('nd,edf->enf', xf, W1) + b1[:, None, :], approximate=False)
        y = jnp.einsum('enf,efd->end', h, W2) + b2[:, None, :]
        w_dense = jnp.zeros((N, E), x.dtype).at[jnp.arange(N)[:, None], top_i].add(top_w)
        out = jnp.einsum('ne,end->nd', w_dense, y).reshape(B, S, D)
        out = _layer_norm(out + x, gamma, beta)
        return out

    def _L1_gnn_ref(x, edge_index, W, a):
        import jax, jax.numpy as jnp
        import numpy as np
        ALPHA = 0.2
        N_NODES = 3125
        N_EDGES = 50000
        NFEAT = 256
        HID = 64
        NHEADS = 4

        def _gat_head(x, src, dst, Wh, ah, n_nodes):
            hid = Wh.shape[1]
            h = x @ Wh
            h = jnp.where(jnp.isnan(h), 0.0, h)
            a1, a2 = (ah[0, :hid], ah[0, hid:])
            alpha_src = h @ a1
            alpha_dst = h @ a2
            s = alpha_src[src] + alpha_dst[dst]
            e = jnp.exp(-jax.nn.leaky_relu(s, ALPHA))
            e = jnp.where(jnp.isnan(e), 0.0, e)
            rowsum = jax.ops.segment_sum(e, src, num_segments=n_nodes)
            hp = jax.ops.segment_sum(e[:, None] * h[dst], src, num_segments=n_nodes)
            hp = jnp.where(jnp.isnan(hp), 0.0, hp)
            hp = hp / rowsum[:, None]
            hp = jnp.where(jnp.isnan(hp), 0.0, hp)
            return jax.nn.elu(hp)
        n_nodes = x.shape[0]
        src, dst = (edge_index[0], edge_index[1])
        outs = [_gat_head(x, src, dst, W[h], a[h], n_nodes) for h in range(W.shape[0])]
        out = jnp.concatenate(outs, axis=1)
        return jax.nn.elu(out)

    def _L1_mix_ref(x, Wqkv, Wproj, bproj, ln_g, ln_b, Wg1, bg1, Wg2, bg2):
        import jax, jax.numpy as jnp
        import numpy as np
        B, N, C, H = (8, 512, 256, 8)
        D = C // H
        GH = C // 4
        b, n, c = x.shape
        h, d = (H, D)
        qkv = (x @ Wqkv).reshape(b, n, 3, h, d)
        q, k, v = (qkv[:, :, 0], qkv[:, :, 1], qkv[:, :, 2])
        k = jax.nn.softmax(k, axis=1)
        context = jnp.einsum('bnhd,bnhv->bhdv', k, v)
        out = jnp.einsum('bnhd,bhdv->bnhv', q, context).reshape(b, n, c)
        mu = jnp.mean(x, axis=-1, keepdims=True)
        var = jnp.var(x, axis=-1, keepdims=True)
        xn = (x - mu) * jax.lax.rsqrt(var + 1e-05) * ln_g + ln_b
        hgate = jax.nn.gelu(xn @ Wg1 + bg1, approximate=False)
        gate = jax.nn.sigmoid(hgate @ Wg2 + bg2)
        return out * gate @ Wproj + bproj

    def _L1_ffn_ref(h, gate_w, gate_b, w1, b1, w2, b2):
        import math
        import jax, jax.numpy as jnp
        import numpy as np
        CAPACITY_FACTOR = 1.25
        B, L, D = h.shape
        E = gate_w.shape[1]
        T = B * L
        C = max(1, math.ceil(CAPACITY_FACTOR * T / E))
        x = h.reshape(T, D)
        logits = x @ gate_w + gate_b
        probs = jax.nn.softmax(logits, axis=-1)
        idx = jnp.argmax(probs, axis=-1)
        prb = jnp.take_along_axis(probs, idx[:, None], axis=1)[:, 0]
        one_hot = jax.nn.one_hot(idx, E, dtype=jnp.float32)
        pos = (jnp.cumsum(one_hot, axis=0) * one_hot).sum(-1).astype(jnp.int32) - 1
        kept = pos < C
        pos_safe = jnp.where(kept, pos, C)
        buf = jnp.zeros((E, C, D), dtype=h.dtype).at[idx, pos_safe].set(x, mode='drop')
        hmid = jax.nn.relu(jnp.einsum('ecd,edf->ecf', buf, w1) + b1[:, None, :])
        ybuf = jnp.einsum('ecf,efd->ecd', hmid, w2) + b2[:, None, :]
        pos_g = jnp.minimum(pos, C - 1)
        y_tok = ybuf[idx, pos_g] * (prb * kept)[:, None]
        y = y_tok.reshape(B, L, D)
        y = jnp.nan_to_num(y, nan=0.0, posinf=10000.0, neginf=-10000.0)
        return y
    edge_index = jnp.stack([src, dst])
    xn = _layernorm(x, axis=-1)
    x = x + _L0_gnn_ref(xn, edge_attr_128, edge_index, L0_gnn_W1w, L0_gnn_W1b, L0_gnn_W2w, L0_gnn_W2b, L0_gnn_W3w, L0_gnn_W3b, L0_gnn_aVw, L0_gnn_aVb, L0_gnn_aEw, L0_gnn_aEb) + _L0_mix_ref(xn[None], L0_mix_W_qkv, L0_mix_W_out, L0_mix_b_out)[0]
    x = x + _L0_ffn_ref(_layernorm(x, axis=-1)[None], L0_ffn_Wr, L0_ffn_br, L0_ffn_W1, L0_ffn_b1, L0_ffn_W2, L0_ffn_b2, L0_ffn_gamma, L0_ffn_beta)[0]
    xn = _layernorm(x, axis=-1)
    x = x + _L1_gnn_ref(xn, edge_index, L1_gnn_W, L1_gnn_a) + _L1_mix_ref(xn[None], L1_mix_Wqkv, L1_mix_Wproj, L1_mix_bproj, L1_mix_ln_g, L1_mix_ln_b, L1_mix_Wg1, L1_mix_bg1, L1_mix_Wg2, L1_mix_bg2)[0]
    x = x + _L1_ffn_ref(_layernorm(x, axis=-1)[None], L1_ffn_gate_w, L1_ffn_gate_b, L1_ffn_w1, L1_ffn_b1, L1_ffn_w2, L1_ffn_b2)[0]
    return x

_drawn_inputs = setup_inputs


def setup_inputs(seed=0):
    import zlib

    import numpy as np

    out = dict(_drawn_inputs(seed))
    spreads = {'L0_mix_b_out': (0.0, 0.1),
     'L0_ffn_br': (0.0, 0.8),
     'L0_ffn_b1': (0.0, 0.305),
     'L0_ffn_b2': (0.0, 0.1),
     'L0_ffn_gamma': (1.0, 0.2),
     'L0_ffn_beta': (0.0, 0.1),
     'L1_mix_bproj': (0.0, 0.684),
     'L1_mix_ln_g': (1.0, 0.6),
     'L1_mix_ln_b': (0.0, 0.8),
     'L1_mix_bg1': (0.0, 0.8),
     'L1_mix_bg2': (0.0, 0.8),
     'L1_ffn_gate_b': (0.0, 0.587),
     'L1_ffn_b1': (0.0, 2.0),
     'L1_ffn_b2': (0.0, 2.0)}
    factors = {'edge_attr_128': 8.0,
     'L0_gnn_W1w': 8.0,
     'L0_gnn_W1b': 6.179,
     'L0_gnn_W2w': 8.0,
     'L0_gnn_W2b': 8.0,
     'L0_gnn_W3b': 5.114,
     'L0_gnn_aVw': 8.0,
     'L0_gnn_aVb': 64.0,
     'L0_gnn_aEw': 8.0,
     'L0_gnn_aEb': 64.0,
     'L1_mix_Wqkv': 6.587,
     'L1_mix_Wproj': 6.963,
     'L1_mix_Wg1': 8.0,
     'L1_mix_Wg2': 8.0,
     'L1_ffn_w1': 4.402,
     'L1_ffn_w2': 3.016}
    for name, (base, spread) in spreads.items():
        noise = np.random.default_rng([zlib.crc32(name.encode()), seed]).standard_normal(out[name].shape)
        drawn = base * np.exp(spread * noise) if base else spread * noise
        out[name] = jnp.asarray(drawn.astype(out[name].dtype))
    for name, factor in factors.items():
        out[name] = (out[name] * factor).astype(out[name].dtype)
    return out
```

```python
import concourse.bass as bass
from concourse import mybir
from contextlib import ExitStack

F32 = mybir.dt.float32
BF16 = mybir.dt.bfloat16
I32 = mybir.dt.int32
U32 = mybir.dt.uint32
ALU = mybir.AluOpType
ACT = mybir.ActivationFunctionType
AX = mybir.AxisListType

P = 128
D = 256
DE = 128
N = 3125
E = 50000
TN = 125
NT = N // TN
DB = D // P
CH = 8
ET = 392
NCH = ET // CH
LASTP = E - (P - 1) * ET
FULLCH = LASTP // CH
GT = 2
GE = GT * P
NG = -(-((E + NT * (GE - 1)) // GE) // 8) * 8
ST = NG * GT
SLOTS = ST * P
ROW = 136
C_ONE, C_SC, C_NID, C_DST = DE, DE + 1, DE + 5, DE + 6
NB = 4
TB = ST // NB
XROW = 260
HROW = 264
NEG = -1.0e30
EPS = 1e-5
XP = 8
F0 = 512
F1 = 1024
CAP = 489
MAGIC = 12582912.0

assert TN * NT == N and LASTP % CH == 0 and ST % 16 == 0


class Steps:

    def __init__(self, eng, sem, start=0):
        self.eng, self.sem, self.start, self.n = eng, sem, start, 0

    def __call__(self, ins):
        ins.then_inc(self.sem, 1)
        self.n += 1

    def settle(self):
        self.eng.wait_ge(self.sem, self.start + self.n)


class Shared:
    pass


class Context:

    def __init__(self, kv, qt, out, inv_scale):
        self.kv, self.qt, self.out, self.inv_scale = kv, qt, out, inv_scale


def alloc(nc, ctx):
    def sb(name, shape, dt=F32):
        return ctx.enter_context(nc.sbuf_tensor(name, shape, dt))

    sems = []

    def finish():
        if sems:
            nc.clear_and_free_semaphores(sems)
            nc.all_engine_barrier()

    ctx.callback(finish)

    def sem(name):
        sems.append(nc.alloc_semaphore(name=name))
        return sems[-1]

    return sb, sem


def setup(nc, g):
    ZW = 56
    with ExitStack() as ctx:
        sb, sem = alloc(nc, ctx)
        zero = sb("zero", [P, ZW * ROW])
        zeroed, built, loaded, cleared = sem("zeroed"), sem("built"), sem("loaded"), sem("cleared")
        sorted_v = g.sorted.rearrange("(p r) c -> p (r c)", p=P)
        xbuf_v = g.xbuf.rearrange("r c -> (r c)").rearrange("(p f) -> p f", p=P)
        with nc.Block() as block:
            @block.vector
            def _(v):
                v.memset(zero[:, :], 0.0).then_inc(zeroed, 1)
                v.memset(g.ones[:, :], 1.0).then_inc(zeroed, 1)

            @block.gpsimd
            def _(pool):
                st = Steps(pool, built)
                st(pool.iota(g.iota[:, :], [[1, P]], base=0, channel_multiplier=0,
                             allow_small_or_imprecise_dtypes=True))
                st(pool.iota(g.part[:, :], [[0, 1]], base=0, channel_multiplier=1,
                             allow_small_or_imprecise_dtypes=True))
                pool.wait_ge(zeroed, 2)
                st(pool.affine_select(out=g.ident[:, :], in_=g.ones[:, :], compare_op=ALU.is_equal, fill=0.0,
                                      base=0, pattern=[[-1, P]], channel_multiplier=1))
                st(pool.affine_select(out=g.before[:, :], in_=g.ones[:, :], compare_op=ALU.is_gt, fill=0.0,
                                      base=0, pattern=[[-1, P]], channel_multiplier=1))
                st(pool.affine_select(out=g.after[:, :], in_=g.ones[:, :], compare_op=ALU.is_gt, fill=0.0,
                                      base=0, pattern=[[1, P]], channel_multiplier=-1))
                st(pool.affine_select(out=g.heads[:, :], in_=g.ones[:, :], compare_op=ALU.is_ge, fill=0.0,
                                      base=0, pattern=[[-32, 4], [0, 32]], channel_multiplier=1))
                st.settle()
                st(pool.affine_select(out=g.heads[:, :], in_=g.heads[:, :], compare_op=ALU.is_ge, fill=0.0,
                                      base=31, pattern=[[32, 4], [0, 32]], channel_multiplier=-1))
                st.settle()

            @block.sync
            def _(sp):
                sp.dma_start(g.X[:, :, :], g.x.rearrange("(j p) d -> p j d", p=TN)).then_inc(loaded, 16)
                sp.wait_ge(zeroed, 1)
                w = ZW * ROW
                for i in range(ST // ZW):
                    sp.dma_start(sorted_v[:, i * w:(i + 1) * w], zero[:, :]).then_inc(cleared, 16)
                w = XP * CAP * D // P // 2
                for i in range(2):
                    sp.dma_start(xbuf_v[:, i * w:(i + 1) * w], zero[:, 0:w]).then_inc(cleared, 16)
                sp.wait_ge(loaded, 16)
                sp.wait_ge(cleared, 16 * (ST // ZW + 2))


def layer_norm(nc, g, src, dst, name, T=None, gain=None, bias=None):
    K, Q = 5, 4
    parts = [(k, a, min(a + Q, NT)) for a in range(0, NT, Q) for k in range(DB)] if T is not None else []
    with ExitStack() as ctx:
        sb, sem = alloc(nc, ctx)
        stats = sb(f"{name}_stats", [TN, NT, 6])
        mean = sb(f"{name}_mean", [TN, NT])
        diff = sb(f"{name}_diff", [TN, NT])
        var = sb(f"{name}_var", [TN, NT])
        own, var_ready, std_ready, normed, turned, copied = (
            sem(f"{name}_{x}") for x in ("own", "var_ready", "std_ready", "normed", "turned", "copied"))
        with nc.Block() as block:
            @block.vector
            def _(v):
                st = Steps(v, own)

                def spread(c):
                    s = slice(K * c, K * c + K)
                    for j in range(K * c, K * c + K):
                        st(v.bn_stats(stats[:, j, :], src[:, j, :]))
                    st.settle()
                    st(v.tensor_tensor(mean[:, s], stats[:, s, 1], stats[:, s, 4], ALU.add))
                    st(v.tensor_tensor(diff[:, s], stats[:, s, 1], stats[:, s, 4], ALU.subtract))
                    st(v.tensor_tensor(var[:, s], stats[:, s, 2], stats[:, s, 5], ALU.add))
                    st.settle()
                    st(v.tensor_scalar(mean[:, s], mean[:, s], 0.5, None, ALU.mult))
                    st(v.tensor_scalar(var[:, s], var[:, s], 1.0 / D, EPS, ALU.mult, ALU.add))
                    st(v.tensor_tensor(diff[:, s], diff[:, s], diff[:, s], ALU.mult))
                    st.settle()
                    v.scalar_tensor_tensor(var[:, s], diff[:, s], 0.25, var[:, s], ALU.mult, ALU.add).then_inc(var_ready, 1)

                def scale(c):
                    s = slice(K * c, K * c + K)
                    v.wait_ge(std_ready, c + 1)
                    st(v.reciprocal(var[:, s], var[:, s]))
                    st.settle()
                    for j in range(K * c, K * c + K):
                        v.tensor_scalar(dst[:, j, 0:D], src[:, j, :], mean[:, j:j + 1], var[:, j:j + 1], ALU.subtract,
                                        ALU.mult).then_inc(normed, 1)

                for c in range(NT // K + 1):
                    if c < NT // K:
                        spread(c)
                    if c >= 1:
                        scale(c - 1)
                v.wait_ge(normed, NT)

            @block.scalar
            def _(act):
                def copy(i):
                    k, a, b = parts[i]
                    act.wait_ge(turned, i + 1)
                    o, t = T[:, k, a * TN:b * TN], g.ps[i % 8][:, 0:(b - a) * TN]
                    if gain is None:
                        act.copy(o, t).then_inc(copied, 1)
                    else:
                        act.activation(o, t, ACT.Identity, bias=bias[:, k:k + 1], scale=gain[:, k:k + 1]).then_inc(copied, 1)

                n = 0
                for c in range(NT // K):
                    s = slice(K * c, K * c + K)
                    act.wait_ge(var_ready, c + 1)
                    act.activation(var[:, s], var[:, s], ACT.Sqrt).then_inc(std_ready, 1)
                    while n < len(parts) and parts[n][2] <= K * (c - 1):
                        copy(n)
                        n += 1
                for i in range(n, len(parts)):
                    copy(i)
                act.wait_ge(copied, len(parts))

            @block.tensor
            def _(pe):
                for i, (k, a, b) in enumerate(parts):
                    pe.wait_ge(normed, b)
                    if i >= 8:
                        pe.wait_ge(copied, i - 7)
                    for j in range(a, b):
                        last = pe.transpose(g.ps[i % 8][:, (j - a) * TN:(j - a + 1) * TN], dst[:, j, k * P:(k + 1) * P],
                                            g.ident[0:TN, 0:TN])
                    last.then_inc(turned, 1)


def turn(nc, g, src, dst, name):
    Q = 4
    parts = [(k, a, min(a + Q, NT)) for a in range(0, NT, Q) for k in range(DB)]
    with ExitStack() as ctx:
        sb, sem = alloc(nc, ctx)
        turned, copied_v, copied_a = (sem(f"{name}_{x}") for x in ("turned", "copied_v", "copied_a"))
        with nc.Block() as block:
            @block.tensor
            def _(pe):
                for i, (k, a, b) in enumerate(parts):
                    if i >= 8:
                        pe.wait_ge((copied_v, copied_a)[i % 2], i // 2 - 3)
                    for j in range(a, b):
                        last = pe.transpose(g.ps[i % 8][:, (j - a) * TN:(j - a + 1) * TN], src[:, j, k * P:(k + 1) * P],
                                            g.ident[0:TN, 0:TN])
                    last.then_inc(turned, 1)

            @block.vector
            def _(v):
                for i, (k, a, b) in enumerate(parts):
                    if i % 2 == 0:
                        v.wait_ge(turned, i + 1)
                        o, t = dst[:, k, a * TN:b * TN], g.ps[i % 8][:, 0:(b - a) * TN]
                        v.tensor_copy(o, t).then_inc(copied_v, 1)
                v.wait_ge(copied_v, len(parts) // 2)

            @block.scalar
            def _(act):
                for i, (k, a, b) in enumerate(parts):
                    if i % 2 == 1:
                        act.wait_ge(turned, i + 1)
                        o, t = dst[:, k, a * TN:b * TN], g.ps[i % 8][:, 0:(b - a) * TN]
                        act.copy(o, t).then_inc(copied_a, 1)
                act.wait_ge(copied_a, len(parts) // 2)


def gnn0_weights(nc, g):
    with ExitStack() as ctx:
        sb, sem = alloc(nc, ctx)
        w1 = sb("w1", [P, 2, DB, D])
        w2 = sb("w2", [P, 2, DE])
        w3t = sb("w3t", [P, 2, 5, D])
        cols = sb("cols", [P, 24])
        rows = sb("rows", [1, 2 * D + 4])
        av = cols[:, 0:16].rearrange("p (h b c) -> p h b c", h=2, b=DB)
        ae, b1, b2 = cols[:, 16:18], cols[:, 18:22].rearrange("p (h b) -> p h b", h=2), cols[:, 22:24]
        b3, ab = rows[:, 0:2 * D].rearrange("p (h d) -> p h d", h=2), rows[:, 2 * D:2 * D + 4]
        asum = sb("asum", [P, 2, DB, 2])
        loaded, formed, taken, own = (sem(f"w0_{x}") for x in ("loaded", "formed", "taken", "own"))
        with nc.Block() as block:
            @block.sync
            def _(sp):
                sp.dma_start(w3t[:, :, :, :], g.w3t).then_inc(loaded, 16)
                sp.dma_start(w1[:, :, :, :], g.w1_0).then_inc(loaded, 16)
                sp.dma_start(w2[:, :, :], g.w2_0).then_inc(loaded, 16)
                sp.dma_start(cols[:, :], g.cols0).then_inc(loaded, 16)
                sp.dma_start(rows[:, :], g.rows0).then_inc(loaded, 16)

            @block.tensor
            def _(pe):
                pe.wait_ge(loaded, 16 * 5)
                n = 0

                def bank():
                    if n >= 4:
                        pe.wait_ge(taken, n - 3)
                    return g.ps[4 + n % 4]

                for h in range(2):
                    for i in range(DB):
                        out = bank()
                        for o in range(DB):
                            last = pe.matmul(out[:, 0:D], w1[:, h, o, i * P:(i + 1) * P], w3t[:, h, o, :],
                                             start=o == 0, stop=o == DB - 1)
                        last.then_inc(formed, 1)
                        n += 1
                    out = bank()
                    pe.matmul(out[:, 0:D], w2[:, h, :], w3t[:, h, 2, :], start=True, stop=True).then_inc(formed, 1)
                    n += 1
                    for i in range(DB):
                        out = bank()
                        for o in range(DB):
                            last = pe.matmul(out[:, 0:4], w1[:, h, o, i * P:(i + 1) * P], av[:, h, o, :],
                                             start=o == 0, stop=o == DB - 1)
                        last.then_inc(formed, 1)
                        n += 1
                    out = bank()
                    pe.matmul(out[:, 0:DE], ae[:, h:h + 1].to_broadcast([P, P]), w2[:, h, :], start=True, stop=True)\
                        .then_inc(formed, 1)
                    n += 1
                out = bank()
                for h in range(2):
                    for o in range(DB):
                        pe.matmul(out[0:1, 0:D], b1[:, h, o:o + 1], w3t[:, h, o, :], start=h + o == 0, stop=False)
                    pe.matmul(out[0:1, 0:D], b2[:, h:h + 1], w3t[:, h, 2, :], start=False, stop=False)
                    last = pe.matmul(out[0:1, 0:D], g.ones[0:1, 0:1], b3[:, h, :], start=False, stop=h == 1)
                last.then_inc(formed, 1)
                n += 1
                for h in range(2):
                    out = bank()
                    pe.wait_ge(own, 1)
                    for o in range(DB):
                        last = pe.matmul(out[0:1, 0:2], b1[:, h, o:o + 1], asum[:, h, o, :], start=o == 0, stop=o == DB - 1)
                    last.then_inc(formed, 1)
                    n += 1
                    out = bank()
                    pe.matmul(out[0:1, 0:1], b2[:, h:h + 1], ae[:, h:h + 1], start=True, stop=True).then_inc(formed, 1)
                    n += 1

            @block.vector
            def _(v):
                v.wait_ge(loaded, 16 * 5)
                st = Steps(v, own)
                avv = av.rearrange("p h b (t s) -> p (h b) t s", s=2)
                st(v.tensor_tensor(asum[:, :, :, :].rearrange("p h b t -> p (h b) t"), avv[:, :, :, 0], avv[:, :, :, 1],
                                   ALU.add))
                n = 0

                def bank():
                    v.wait_ge(formed, n + 1)
                    return g.ps[4 + n % 4]

                for h in range(2):
                    for i in range(DB):
                        v.tensor_scalar(g.G[:, h, i, :], bank()[:, 0:D], 0.5, None, ALU.mult).then_inc(taken, 1)
                        n += 1
                    v.tensor_scalar(g.Q[:, h, :], bank()[:, 0:D], 0.5, None, ALU.mult).then_inc(taken, 1)
                    n += 1
                    for i in range(DB):
                        v.tensor_copy(g.A8[:, i, :].rearrange("p (s t h) -> p h t s", s=2, t=2)[:, h],
                                      bank()[:, 0:4].rearrange("p (t s) -> p t s", s=2)).then_inc(taken, 1)
                        n += 1
                    v.tensor_copy(g.ge[:, h, :], bank()[:, 0:DE]).then_inc(taken, 1)
                    n += 1
                v.tensor_scalar(g.bc[:, :], bank()[0:1, 0:D], 0.5, None, ALU.mult).then_inc(taken, 1)
                n += 1
                for i in range(DB):
                    st(v.tensor_tensor(g.WC[:, i, :], w3t[:, 0, 3 + i, :], w3t[:, 1, 3 + i, :], ALU.add))
                st(v.memset(g.c8[:, :], 0.0))
                st.settle()
                st(v.tensor_scalar(g.WC[:, :, :], g.WC[:, :, :], 0.5, None, ALU.mult))
                c8 = g.c8[:, 0:4].rearrange("p (t h) -> p h t", h=2)
                abv = ab.rearrange("p (t h) -> p h t", h=2)
                for h in range(2):
                    v.tensor_tensor(c8[:, h], bank()[0:1, 0:2], abv[:, h], ALU.add).then_inc(taken, 1)
                    n += 1
                    v.wait_ge(taken, n)
                    v.tensor_tensor(c8[:, h, 1:2], c8[:, h, 1:2], bank()[0:1, 0:1], ALU.add).then_inc(taken, 1)
                    n += 1
                v.wait_ge(taken, n)
                st.settle()


def node_scores(nc, g):
    with ExitStack() as ctx:
        sb, sem = alloc(nc, ctx)
        formed, taken, stored, pv_ready = (sem(f"ns_{x}") for x in ("formed", "taken", "stored", "pv_ready"))
        tabv = sb("tabv", [TN, NT, 4])
        with nc.Block() as block:
            @block.tensor
            def _(pe):
                for j in range(NT):
                    for k in range(DB):
                        pe.matmul(g.ps[0][0:TN, 8 * j:8 * j + 8], g.XNT[:, k, j * TN:(j + 1) * TN], g.A8[:, k, :],
                                  start=k == 0, stop=False)
                    last = pe.matmul(g.ps[0][0:TN, 8 * j:8 * j + 8], g.ones[0:1, 0:TN], g.c8[:, :], start=False, stop=True)
                last.then_inc(formed, 1)

            @block.vector
            def _(v):
                v.wait_ge(formed, 1)
                s = g.ps[0][0:TN, 0:8 * NT].rearrange("p (j c) -> p j c", c=8)
                v.tensor_copy(tabv[:, :, :], s[:, :, 4:8]).then_inc(pv_ready, 1)
                v.tensor_copy(g.tabu[:, :, :], s[:, :, 0:4].rearrange("p j c -> p c j")).then_inc(taken, 1)
                v.wait_ge(taken, 1)
                v.memset(g.XN[:, :, D:XROW], 1.0).then_inc(taken, 1)
                v.wait_ge(taken, 2)

            @block.sync
            def _(sp):
                sp.wait_ge(pv_ready, 1)
                sp.dma_start(g.pvd.rearrange("(j p) c -> p j c", p=TN), tabv[:, :, :]).then_inc(stored, 16)
                sp.wait_ge(taken, 2)
                sp.dma_start(g.xnd.rearrange("(j p) c -> p j c", p=TN), g.XN[:, :, :]).then_inc(stored, 16)
                sp.wait_ge(stored, 32)


def digits(nc, g):
    with ExitStack() as ctx:
        sb, sem = alloc(nc, ctx)
        srci = sb("srci", [P, ET], I32)
        cleared, loaded, own = sem("dg_cleared"), sem("dg_loaded"), sem("dg_own")
        with nc.Block() as block:
            @block.vector
            def _(v):
                st = Steps(v, own)
                v.memset(srci[:, :], N).then_inc(cleared, 1)
                v.memset(g.dsti[:, :], 0).then_inc(cleared, 1)
                v.wait_ge(loaded, 64)
                st(v.tensor_copy(g.srcf, srci[:, :]))
                st(v.tensor_copy(g.dstf[:, :], g.dsti[:, :]))
                st.settle()
                st(v.tensor_scalar(g.hi[:, :], g.srcf, 0.5, 1.0 / TN, ALU.add, ALU.mult))
                st.settle()
                st(v.tensor_scalar(g.hi[:, :], g.hi[:, :], 0.5, MAGIC, ALU.subtract, ALU.add))
                st.settle()
                st(v.tensor_scalar(g.hi[:, :], g.hi[:, :], MAGIC, None, ALU.subtract))
                st.settle()
                st(v.scalar_tensor_tensor(g.lo, g.hi[:, :], -float(TN), g.srcf, ALU.mult, ALU.add))
                st.settle()

            @block.sync
            def _(sp):
                sp.wait_ge(cleared, 2)
                cut = (P - 1) * ET
                for t, f in ((srci, g.src), (g.dsti, g.dst)):
                    sp.dma_start(t[0:P - 1, :], f[0:cut].rearrange("(p t) -> p t", p=P - 1)).then_inc(loaded, 16)
                    sp.dma_start(t[P - 1:P, 0:LASTP], f[cut:E].rearrange("(o t) -> o t", o=1)).then_inc(loaded, 16)
                sp.wait_ge(loaded, 64)


def histogram(nc, g):
    with ExitStack() as ctx:
        sb, sem = alloc(nc, ctx)
        iob = sb("iob", [P, TN], BF16)
        ohl = sb("ohl", [P, 2, CH, TN], BF16)
        ohh = sb("ohh", [P, 2, CH, NT], BF16)
        ready, coded, counted, taken, own = (sem(f"hi_{x}") for x in ("ready", "coded", "counted", "taken", "own"))
        bank_free, gate = sem("hi_bank_free"), sem("hi_gate")

        with nc.Block() as block:
            @block.vector
            def _(v):
                v.tensor_copy(iob[:, :], g.iota[:, 0:TN]).then_inc(ready, 1)
                v.wait_ge(ready, 1)

                def code(c, s, done):
                    v.wait_ge(counted, c + 1)
                    v.tensor_tensor(ohl[:, s], iob[:, :].unsqueeze(1).to_broadcast([P, CH, TN]),
                                    g.lo[:, bass.ds(c * CH, CH)].unsqueeze(2).to_broadcast([P, CH, TN]),
                                    ALU.is_equal).then_inc(coded, 1)
                    v.tensor_tensor(ohh[:, s], g.iota[:, 0:NT].unsqueeze(1).to_broadcast([P, CH, NT]),
                                    g.hi[:, bass.ds(c * CH, CH)].unsqueeze(2).to_broadcast([P, CH, NT]),
                                    ALU.is_equal).then_inc(coded, 1)

                code(0, 0, 0)
                with v.Fori(0, NCH // 2) as i:
                    for s in range(2):
                        code(i * 2 + 1 + s, 1 - s, 0)

            @block.tensor
            def _(pe):
                pe.sem_inc(counted, 2)

                def count(c, s):
                    pe.wait_ge(coded, c * 2 + 2)
                    pe.wait_ge(bank_free, c + 1)
                    for u in range(CH):
                        last = pe.matmul(g.ps[s][0:TN, u * NT:(u + 1) * NT], ohl[:, s, u, :], ohh[:, s, u, :],
                                         start=True, stop=True)
                    last.then_inc(counted, 1)

                count(0, 0)
                with pe.Fori(0, NCH // 2) as i:
                    for s in range(2):
                        count(i * 2 + 1 + s, 1 - s)

            @block.scalar
            def _(act):
                act.sem_inc(bank_free, 2)

                def take(c, s):
                    act.wait_ge(counted, c + 3)
                    act.sem_inc(gate, 1)
                    act.copy(g.hist[:, :, bass.ds(c * CH, CH)].rearrange("p h t -> p t h"),
                             g.ps[s][0:TN, 0:CH * NT].rearrange("p (t h) -> p t h", h=NT)).then_inc(bank_free, 1)

                take(0, 0)
                with act.Fori(0, NCH // 2) as i:
                    for s in range(2):
                        take(i * 2 + 1 + s, 1 - s)
                act.wait_ge(bank_free, NCH + 2)


def places(nc, g):
    with ExitStack() as ctx:
        sb, sem = alloc(nc, ctx)
        zeros = sb("pl_zeros", [TN, ET])
        base = sb("pl_base", [P, NT])
        basei = sb("pl_basei", [P, NT], I32)
        start = sb("pl_start", [TN, NT])
        gidx = sb("pl_gidx", [P, NG])
        gj = sb("pl_gj", [P, NG])
        own, deg_ready, gidx_ready, summed = sem("pl_own"), sem("pl_deg"), sem("pl_gidx"), sem("pl_summed")
        with nc.Block() as block:
            @block.tensor
            def _(pe):
                pe.wait_ge(deg_ready, 1)
                pe.matmul(g.ps[2][:, 0:NT], g.ones[0:TN, :], g.deg[:, :], start=True, stop=True).then_inc(summed, 1)
                pe.matmul(g.ps[3][0:TN, 0:NT], g.after[0:TN, 0:TN], g.deg[:, :], start=True, stop=True).then_inc(summed, 1)

            @block.gpsimd
            def _(pool):
                pool.iota(gidx[:, :], [[GE, NG]], base=0, channel_multiplier=0,
                          allow_small_or_imprecise_dtypes=True).then_inc(gidx_ready, 1)

            @block.vector
            def _(v):
                st = Steps(v, own)
                st(v.memset(zeros[:, :], 0.0))
                st(v.tensor_reduce(g.deg[:, :], g.hist[:, :, :], AX.X, ALU.add))
                st.settle()
                v.sem_inc(deg_ready, 1)
                v.wait_ge(summed, 1)
                st(v.tensor_copy(basei[:, :], g.ps[2][:, 0:NT]))
                st.settle()
                st(v.tensor_single_scalar(basei[:, :], basei[:, :], GE - 1, ALU.add))
                st.settle()
                sh = GE.bit_length() - 1
                st(v.tensor_scalar(basei[:, :], basei[:, :], sh, sh, ALU.arith_shift_right, ALU.arith_shift_left))
                st.settle()
                st(v.tensor_copy(base[:, :], basei[:, :]))
                st.settle()
                st(v.tensor_tensor_scan(g.base[:, :], base[:, :], g.part[:, :].to_broadcast([P, NT]), 0.0, ALU.add, ALU.bypass))
                st.settle()
                st(v.tensor_tensor(g.base[:, :], g.base[:, :], base[:, :], ALU.subtract))
                st.settle()
                v.wait_ge(summed, 2)
                st(v.tensor_tensor(start[:, :], g.ps[3][0:TN, 0:NT], g.base[0:TN, :], ALU.add))
                st.settle()
                for j in range(NT):
                    st(v.tensor_tensor_scan(g.place[:, j, :], g.hist[:, j, :], zeros[:, :], start[:, j:j + 1],
                                            ALU.add, ALU.add))
                v.wait_ge(gidx_ready, 1)
                st(v.tensor_scalar(gj[:, :], gidx[:, :], g.base[:, 1:2], None, ALU.is_ge))
                for j in range(2, NT):
                    st.settle()
                    st(v.scalar_tensor_tensor(gj[:, :], gidx[:, :], g.base[:, j:j + 1], gj[:, :], ALU.is_ge, ALU.add))
                st.settle()
                st(v.tensor_tensor(g.hist[:, :, :], g.place[:, :, :], g.hist[:, :, :], ALU.subtract))
                st(v.tensor_copy(g.gji[:, :], gj[0:1, :]))
                st(v.tensor_scalar(g.gfirst[:, :], gj[:, :], float(TN), 1.0, ALU.mult, ALU.add))
                st.settle()


def locate(nc, g):
    H = 4
    NQ = ET // H
    with ExitStack() as ctx:
        sb, sem = alloc(nc, ctx)
        stage = sb("lc_stage", [P, 2, 2, H])
        oht = sb("lc_oht", [TN, 2, H * P])
        ohh = sb("lc_ohh", [P, 2, H, NT])
        rank = sb("lc_rank", [P, 2, H])
        ranks = sb("lc_ranks", [P, ET])
        same = sb("lc_same", [P, 2, H, P])
        picked = sb("lc_picked", [P, H, 5, NT])
        idx = sb("lc_idx", [P, 2, CH], I32)
        pv = sb("lc_pv", [P, 2, CH, 4])
        staged, turned, coded, rows_free, looked, table_free, own = (
            sem(f"lc_{x}") for x in ("staged", "turned", "coded", "rows_free", "looked", "table_free", "own"))
        idx_ready, pv_free, pool_gate, act_gate = (sem(f"lc_{x}") for x in ("idx_ready", "pv_free", "pgate", "agate"))
        got = [[sem(f"lc_got{s}_{u}") for u in range(CH)] for s in range(2)]

        with nc.Block() as block:
            @block.vector
            def _(v):
                def put(q, h):
                    v.tensor_copy(stage[:, h], g.sl[:, :, bass.ds(q * H, H)]).then_inc(staged, 1)

                def encode(st, q, h):
                    v.wait_ge(turned, q + 1)
                    v.tensor_scalar(oht[:, h, :], g.ps[2 + h][0:TN, :], g.part[0:TN, :], None,
                                    ALU.is_equal).then_inc(coded, 1)
                    for u in range(H):
                        ins = v.scalar_tensor_tensor(same[:, h, u, :], g.ps[h][:, u * P:(u + 1) * P], stage[:, h, 0, u:u + 1],
                                                     g.before[:, :], ALU.is_equal, ALU.mult, accum_out=rank[:, h, u:u + 1])
                        st(ins)
                    st(v.tensor_tensor(ohh[:, h], g.iota[:, 0:NT].unsqueeze(1).to_broadcast([P, H, NT]),
                                       g.hi[:, bass.ds(q * H, H)].unsqueeze(2).to_broadcast([P, H, NT]), ALU.is_equal))

                def select(st, q, h):
                    st.settle()
                    v.sem_inc(rows_free, 1)
                    v.wait_ge(looked, q + 1)
                    st(v.tensor_tensor(picked[:, :, :, :], g.ps[4 + h][:, 0:H * 5 * NT].rearrange("p (u c j) -> p u c j", u=H, c=5),
                                       ohh[:, h].unsqueeze(2).to_broadcast([P, H, 5, NT]), ALU.mult))
                    st(v.tensor_copy(ranks[:, bass.ds(q * H, H)], rank[:, h]))
                    st.settle()
                    v.sem_inc(table_free, 1)
                    st(v.tensor_reduce(g.found[:, bass.ds(q * H, H), :], picked[:, :, :, :], AX.X, ALU.add))
                    st.settle()

                K = H + 1 + 3
                put(0, 0)
                put(1, 1)
                st = Steps(v, own)
                encode(st, 0, 0)
                st.settle()
                with v.Fori(0, NQ // 2 - 1) as i:
                    for s in range(2):
                        q = i * 2 + 1 + s
                        put(q + 1, s)
                        st = Steps(v, own, (q - 1) * K + H + 1)
                        encode(st, q, 1 - s)
                        select(st, q - 1, s)
                        assert st.n == K
                st = Steps(v, own, (NQ - 2) * K + H + 1)
                encode(st, NQ - 1, 1)
                select(st, NQ - 2, 0)
                select(st, NQ - 1, 1)
                st(v.tensor_tensor(ranks[:, :], ranks[:, :], g.found[:, :, 0], ALU.add))
                st.settle()
                st(v.tensor_scalar(g.found[:, :, 0], g.sl[:, 0, :], float(N), 4.0 * SLOTS, ALU.is_ge, ALU.mult))
                st.settle()
                st(v.tensor_tensor(g.slot[:, :], ranks[:, :], g.found[:, :, 0], ALU.add))
                st.settle()

            @block.tensor
            def _(pe):
                def rows(q, h):
                    pe.wait_ge(staged, q + 1)
                    pe.wait_ge(rows_free, q + 1)
                    for u in range(H):
                        pe.transpose(g.ps[h][:, u * P:(u + 1) * P], stage[:, h, 0, u:u + 1].to_broadcast([P, P]), g.ident[:, :])
                    for u in range(H):
                        last = pe.transpose(g.ps[2 + h][0:TN, u * P:(u + 1) * P], stage[:, h, 1, u:u + 1].to_broadcast([P, TN]),
                                            g.ident[:, :])
                    last.then_inc(turned, 1)

                def look(q, h):
                    pe.wait_ge(coded, q + 1)
                    pe.wait_ge(table_free, q + 1)
                    for u in range(H):
                        lhs = oht[:, h, u * P:(u + 1) * P]
                        o = u * 5 * NT
                        pe.matmul(g.ps[4 + h][:, o + NT:o + 5 * NT], lhs, g.tabu[:, :, :].rearrange("p c j -> p (c j)"),
                                  start=True, stop=True)
                        last = pe.matmul(g.ps[4 + h][:, o:o + NT], lhs, g.hist[:, :, bass.ds(q * H + u, 1)]
                                         .rearrange("p j o -> p (j o)"), start=True, stop=True)
                    last.then_inc(looked, 1)

                pe.sem_inc(rows_free, 2)
                pe.sem_inc(table_free, 2)
                rows(0, 0)
                with pe.Fori(0, NQ // 2 - 1) as i:
                    for s in range(2):
                        q = i * 2 + 1 + s
                        rows(q, 1 - s)
                        look(q - 1, s)
                rows(NQ - 1, 1)
                look(NQ - 2, 0)
                look(NQ - 1, 1)

            @block.scalar
            def _(act):
                act.sem_inc(pv_free, 2)

                def put(c, s):
                    act.copy(idx[:, s], g.dsti[:, bass.ds(c * CH, CH)]).then_inc(idx_ready, 1)

                def collect(c, s, uses):
                    for u in range(CH):
                        act.wait_ge(got[s][u], uses * 16)
                    act.sem_inc(act_gate, 1)
                    act.copy(g.pv[:, bass.ds(c * CH, CH), :], pv[:, s]).then_inc(pv_free, 1)

                put(0, 0)
                put(1, 1)
                collect(0, 0, 1)
                with act.Fori(0, NCH // 2 - 1) as i:
                    for s in range(2):
                        c = i * 2 + 1 + s
                        put(c + 1, s)
                        collect(c, 1 - s, i + 1 + s)
                put(NCH - 1, 0)
                collect(NCH - 2, 1, NCH // 2)
                collect(NCH - 1, 0, NCH // 2 + 1)
                act.wait_ge(pv_free, NCH + 2)

            @block.gpsimd
            def _(pool):
                def gather(c, s):
                    pool.wait_ge(idx_ready, c + 1)
                    pool.wait_ge(pv_free, c + 1)
                    pool.sem_inc(pool_gate, 1)
                    for u in range(CH):
                        pool.indirect_dma_start(pv[:, s, u, :], None, g.pvd, bass.IndirectOffsetOnAxis(
                            ap=idx[:, s, u:u + 1], axis=0)).then_inc(got[s][u], 16)

                gather(0, 0)
                with pool.Fori(0, NCH // 2) as i:
                    for s in range(2):
                        gather(i * 2 + 1 + s, 1 - s)


def scatter(nc, g):
    with ExitStack() as ctx:
        sb, sem = alloc(nc, ctx)
        row = sb("sc_row", [P, 2, CH, ROW])
        ce = sb("sc_ce", [P, 2, CH])
        s4 = sb("sc_s4", [P, CH, 4])
        junk = sb("sc_junk", [P, CH, 2, DE])
        idx = sb("sc_idx", [P, 2, CH], I32)
        set_up, row_ready, row_free, loaded0, loaded1, own, gate = (
            sem(f"sc_{x}") for x in ("set_up", "row_ready", "row_free", "loaded0", "loaded1", "own", "gate"))
        loaded = (loaded0, loaded1)
        sent = [[sem(f"sc_sent{s}_{u}") for u in range(CH)] for s in range(2)]
        edge_v = g.edge_attr_128[0:(P - 1) * ET].rearrange("(p t) c -> p t c", p=P - 1)
        edge_l = g.edge_attr_128[(P - 1) * ET:E].rearrange("(o t) c -> o t c", o=1)

        with nc.Block() as block:
            @block.sync
            def _(sp):
                sp.wait_ge(set_up, 1)

                def free(uses, s):
                    for u in range(CH):
                        sp.wait_ge(sent[s][u], uses * 16)

                def load(c, s, full):
                    sp.dma_start(row[0:P - 1, s, :, 0:DE], edge_v[:, bass.ds(c * CH, CH), :]).then_inc(loaded[s], 16)
                    if full:
                        sp.dma_start(row[P - 1:P, s, :, 0:DE], edge_l[:, bass.ds(c * CH, CH), :]).then_inc(loaded[s], 16)
                    else:
                        sp.dma_start(row[P - 1:P, s, :, 0:DE], edge_l[:, 0:CH, :]).then_inc(loaded[s], 16)

                load(0, 0, True)
                load(1, 1, True)
                with sp.Fori(0, FULLCH // 2 - 1) as i:
                    for s in range(2):
                        free(i + 1, s)
                        load(i * 2 + 2 + s, s, True)
                n = FULLCH // 2 * 2
                for c in range(n, FULLCH + 1):
                    free(c // 2, c % 2)
                    load(c, c % 2, c < FULLCH)
                assert (FULLCH + 1) % 2 == 0 and NCH % 2 == 1
                with sp.Fori((FULLCH + 1) // 2, NCH // 2) as i:
                    for s in range(2):
                        free(i, s)
                        load(i * 2 + s, s, False)
                free(NCH // 2, 0)
                load(NCH - 1, 0, False)

            @block.vector
            def _(v):
                v.memset(row[:, :, :, :], 0.0).then_inc(own, 1)
                v.wait_ge(own, 1)
                v.memset(row[:, :, :, C_ONE:C_ONE + 1], 1.0).then_inc(own, 1)
                v.wait_ge(own, 2)
                v.sem_inc(set_up, 1)
                K = 2 * CH + 6

                def fill(c, s, uses):
                    st = Steps(v, own, c * K + 2)
                    cs = bass.ds(c * CH, CH)
                    v.wait_ge(loaded[s], uses * 32)
                    for u in range(CH):
                        for h in range(2):
                            st(v.tensor_tensor_reduce(junk[:, u, h, :], row[:, s, u, 0:DE], g.ge[:, h, :], 1.0, 0.0, ALU.mult,
                                                      ALU.add, ce[:, h, u:u + 1]))
                    st(v.tensor_tensor(s4[:, :, :], g.found[:, cs, 1:5], g.pv[:, cs, :], ALU.add))
                    st(v.tensor_copy(row[:, s, :, C_DST:C_DST + 1], g.dstf[:, cs].unsqueeze(2)))
                    st(v.tensor_scalar(row[:, s, :, C_NID:C_NID + 1], g.sl[:, 0, cs].unsqueeze(2), 1.0, None, ALU.add))
                    st(v.tensor_copy(idx[:, s, :], g.slot[:, cs]))
                    st.settle()
                    st(v.tensor_tensor(s4[:, :, 2:4], s4[:, :, 2:4], ce[:, :, :].rearrange("p h u -> p u h"), ALU.add))
                    st.settle()
                    st(v.scalar_tensor_tensor(row[:, s, :, C_SC:C_SC + 4], s4[:, :, :], 0.01, s4[:, :, :], ALU.mult, ALU.max))
                    st.settle()
                    v.sem_inc(row_ready, 1)

                fill(0, 0, 1)
                with v.Fori(0, NCH // 2) as i:
                    for s in range(2):
                        fill(i * 2 + 1 + s, 1 - s, i + 1 + s)

            @block.gpsimd
            def _(pool):
                def send(c, s):
                    pool.wait_ge(row_ready, c + 1)
                    pool.sem_inc(gate, 1)
                    for u in range(CH):
                        pool.indirect_dma_start(g.sorted, bass.IndirectOffsetOnAxis(ap=idx[:, s, u:u + 1], axis=0),
                                                row[:, s, u, :], None, bounds_check=SLOTS - 1,
                                                oob_is_err=False).then_inc(sent[s][u], 16)

                send(0, 0)
                with pool.Fori(0, NCH // 2) as i:
                    for s in range(2):
                        send(i * 2 + 1 + s, 1 - s)
                for s in range(2):
                    for u in range(CH):
                        pool.wait_ge(sent[s][u], 16 * (NCH // 2 + 1 - s))


def edge_weights(nc, g):
    with ExitStack() as ctx:
        sb, sem = alloc(nc, ctx)
        rl = sb("ew_rl", [TB, NB, P, 6])
        reset = sb("ew_reset", [TB, NB, P + 1])
        run = sb("ew_run", [TB, 2, NB, 4, P])
        rows = sb("ew_rows", [4, 2, ST])
        apart = sb("ew_apart", [4, ST + 1])
        many = sb("ew_many", [4, ST])
        pen = sb("ew_pen", [4, 2, ST])
        outof = sb("ew_outof", [4, 2, ST])
        into = sb("ew_into", [4, 2, ST])
        carry = sb("ew_carry", [TB, 2, NB, 4])
        loaded, own, ends_ready, ends_turned, into_ready, into_turned = (
            sem(f"ew_{x}") for x in ("loaded", "own", "ends_ready", "ends_turned", "into_ready", "into_turned"))
        sub_ready, w_ready, w_turned = (sem(f"ew_{x}") for x in ("sub_ready", "w_ready", "w_turned"))
        src = g.sorted.rearrange("(b p s) c -> b p s c", b=NB, p=TB)
        with nc.Block() as block:
            @block.sync
            def _(sp):
                for b in range(NB):
                    sp.dma_start(rl[:, b, :, :], src[b, :, :, C_SC:C_SC + 6]).then_inc(loaded, 16)

            @block.vector
            def _(v):
                st = Steps(v, own)
                st(v.memset(reset[:, :, :], 0.0))
                st(v.memset(apart[:, :], NEG))
                st(v.memset(into[:, :, :], NEG))
                st.settle()
                v.wait_ge(loaded, 16 * NB)
                st(v.tensor_tensor(reset[:, :, 1:P], rl[:, :, 1:P, 4], rl[:, :, 0:P - 1, 4], ALU.not_equal))
                st.settle()
                st(v.tensor_scalar(reset[:, :, 1:P], reset[:, :, 1:P], NEG, None, ALU.mult))
                st.settle()

                def scans(initial):
                    for b in range(NB):
                        for k in range(4):
                            st(v.tensor_tensor_scan(run[:, 0, b, k, :], reset[:, b, 0:P], rl[:, b, :, k],
                                                    initial(0, b, k), ALU.add, ALU.max))
                            st(v.tensor_tensor_scan(run[:, 1, b, k, ::-1], reset[:, b, P:0:-1], rl[:, b, ::-1, k],
                                                    initial(1, b, k), ALU.add, ALU.max))
                    st.settle()

                scans(lambda d, b, k: NEG)
                v.sem_inc(ends_ready, 1)
                v.wait_ge(ends_turned, 1)
                st(v.tensor_copy(rows[:, 0, :], g.ps[2][0:4, 0:ST]))
                st(v.tensor_copy(rows[:, 1, :], g.ps[3][0:4, 0:ST]))
                st.settle()
                st(v.tensor_tensor(apart[:, 1:ST], rows[:, 0, 1:ST], rows[:, 1, 0:ST - 1], ALU.not_equal))
                st(v.tensor_tensor(many[:, :], rows[:, 0, :], rows[:, 1, :], ALU.not_equal))
                st.settle()
                st(v.tensor_scalar(apart[:, 1:ST], apart[:, 1:ST], NEG, None, ALU.mult))
                st(v.tensor_scalar(many[:, :], many[:, :], NEG, None, ALU.mult))
                st.settle()
                st(v.tensor_tensor(pen[:, 0, :], apart[:, 0:ST], many[:, :], ALU.min))
                st(v.tensor_tensor(pen[:, 1, :], apart[:, 1:ST + 1], many[:, :], ALU.min))
                st.settle()
                st(v.tensor_tensor_scan(outof[:, 0, :], pen[:, 0, :], g.ps[0][0:4, 0:ST], NEG, ALU.add, ALU.max))
                st(v.tensor_tensor_scan(outof[:, 1, ::-1], pen[:, 1, ::-1], g.ps[1][0:4, ST - 1::-1], NEG, ALU.add, ALU.max))
                st.settle()
                st(v.tensor_tensor(into[:, 0, 1:ST], outof[:, 0, 0:ST - 1], apart[:, 1:ST], ALU.add))
                st(v.tensor_tensor(into[:, 1, 0:ST - 1], outof[:, 1, 1:ST], apart[:, 1:ST], ALU.add))
                st.settle()
                v.sem_inc(into_ready, 1)
                v.wait_ge(into_turned, 1)
                st(v.tensor_copy(carry[:, :, :, :], g.ps[4][0:TB, 0:8 * NB].rearrange("p (d b k) -> p d b k", d=2, b=NB)))
                st.settle()
                scans(lambda d, b, k: carry[:, d, b, k:k + 1])
                for b in range(NB):
                    st(v.tensor_tensor(run[:, 0, b], run[:, 0, b], run[:, 1, b], ALU.max))
                st.settle()
                for b in range(NB):
                    v.tensor_tensor(run[:, 0, b], rl[:, b, :, 0:4].rearrange("p s k -> p k s"), run[:, 0, b],
                                    ALU.subtract).then_inc(sub_ready, 1)
                for i in range(4):
                    v.wait_ge(w_turned, i + 1)
                    st(v.tensor_copy(g.sw[:, i, :], g.ps[i][:, 0:ST]))
                v.wait_ge(w_turned, 5)
                st(v.tensor_tensor(g.sw[:, 4, :].rearrange("p (g t) -> p g t", t=GT),
                                   g.ps[4][:, 0:ST].rearrange("p (g t) -> p g t", t=GT),
                                   g.gfirst[:, :].unsqueeze(2).to_broadcast([P, NG, GT]), ALU.subtract))
                v.wait_ge(w_turned, 6)
                st(v.tensor_copy(g.sdst[:, :], g.ps[5][:, 0:ST]))
                st.settle()

            @block.scalar
            def _(act):
                for b in range(NB):
                    act.wait_ge(sub_ready, b + 1)
                    act.activation(run[:, 1, b], run[:, 0, b], ACT.Exp).then_inc(w_ready, 1)

            @block.tensor
            def _(pe):
                idt = g.ident[0:TB, 0:TB]
                pe.wait_ge(ends_ready, 1)
                for b in range(NB):
                    o = slice(b * TB, (b + 1) * TB)
                    pe.transpose(g.ps[0][0:4, o], run[:, 0, b, :, P - 1], idt)
                    pe.transpose(g.ps[1][0:4, o], run[:, 1, b, :, 0], idt)
                    pe.transpose(g.ps[2][0:4, o], rl[:, b, 0, 4:5].to_broadcast([TB, 4]), idt)
                    last = pe.transpose(g.ps[3][0:4, o], rl[:, b, P - 1, 4:5].to_broadcast([TB, 4]), idt)
                last.then_inc(ends_turned, 1)
                pe.wait_ge(into_ready, 1)
                for d in range(2):
                    for b in range(NB):
                        c = (d * NB + b) * 4
                        last = pe.transpose(g.ps[4][0:TB, c:c + 4], into[:, d, b * TB:(b + 1) * TB], g.ident[0:4, 0:4])
                last.then_inc(into_turned, 1)
                pe.wait_ge(w_ready, NB)
                for i in range(4):
                    for b in range(NB):
                        last = pe.transpose(g.ps[i][:, b * TB:(b + 1) * TB], run[:, 1, b, i, :], idt)
                    last.then_inc(w_turned, 1)
                for i in range(4, 6):
                    for b in range(NB):
                        last = pe.transpose(g.ps[i][:, b * TB:(b + 1) * TB], rl[:, b, :, i], idt)
                    last.then_inc(w_turned, 1)


def gather_sums0(nc, g):
    U = 4
    NC = ST // U
    R = 4
    W = D + 1 + DE + 1
    with ExitStack() as ctx:
        sb, sem = alloc(nc, ctx)
        idx = sb("a0_idx", [P, R, U], I32)
        xr = sb("a0_xr", [P, R, U, XROW])
        er = sb("a0_er", [P, R, U, DE + 1])
        stg = sb("a0_stg", [P, 2, 5, U])
        oh = sb("a0_oh", [P, 2, U, TN])
        sc = sb("a0_sc", [P, 2, U, 4, TN])
        idx_ready, gate, agate, own = (sem(f"a0_{x}") for x in ("idx_ready", "gate", "agate", "own"))
        oh_ready, sv_ready, se_ready, summed, bank_free = (
            sem(f"a0_{x}") for x in ("oh_ready", "sv_ready", "se_ready", "summed", "bank_free"))
        got = [[sem(f"a0_got{s}_{u}") for u in range(U)] for s in range(R)]
        e_got = [sem(f"a0_egot{s}") for s in range(R)]
        src = g.sorted.rearrange("(t p) c -> p t c", p=P)
        with nc.Block() as block:
            @block.sync
            def _(sp):
                with sp.Fori(0, NC // R) as i:
                    for s in range(R):
                        c = i * R + s
                        sp.wait_ge(summed, c * 2 + 2)
                        sp.dma_start(er[:, s, :, :], src[:, bass.ds(c * U, U), 0:DE + 1]).then_inc(e_got[s], 16)

            @block.gpsimd
            def _(pool):
                with pool.Fori(0, NC // R) as i:
                    for s in range(R):
                        pool.wait_ge(idx_ready, i * R + (s + 1))
                        pool.sem_inc(gate, 1)
                        for u in range(U):
                            pool.indirect_dma_start(xr[:, s, u, :], None, g.xnd, bass.IndirectOffsetOnAxis(
                                ap=idx[:, s, u:u + 1], axis=0)).then_inc(got[s][u], 16)

            @block.scalar
            def _(act):
                def put(c, s):
                    act.wait_ge(summed, c * 2 + 2)
                    act.sem_inc(agate, 1)
                    act.copy(idx[:, s], g.sdst[:, bass.ds(c * U, U)]).then_inc(idx_ready, 1)

                def weigh(c, s):
                    act.wait_ge(oh_ready, c + 1)
                    act.wait_ge(summed, c * 2 + (2 * R - 2))
                    for u in range(U):
                        for k in (2, 3):
                            last = act.activation(sc[:, s, u, k, :], oh[:, s, u, :], ACT.Copy, scale=stg[:, s, k, u:u + 1])
                    last.then_inc(se_ready, 1)

                for c in range(3):
                    put(c, c)
                weigh(0, 0)
                with act.Fori(0, NC // R - 1) as i:
                    for s in range(R):
                        c = i * R + s
                        put(c + 3, (s + 3) % R)
                        weigh(c + 1, (s + 1) % 2)
                for c in range(NC - R, NC):
                    if c + 1 < NC:
                        weigh(c + 1, (c + 1) % 2)
                    if c + 3 < NC:
                        put(c + 3, (c + 3) % R)

            @block.vector
            def _(v):
                def build(st, c, s):
                    v.wait_ge(summed, c * 2 + (2 * R - 2))
                    st(v.tensor_copy(stg[:, s], g.sw[:, :, bass.ds(c * U, U)]))
                    st.settle()
                    st(v.tensor_tensor(oh[:, s], g.iota[:, 0:TN].unsqueeze(1).to_broadcast([P, U, TN]),
                                       stg[:, s, 4, :].unsqueeze(2).to_broadcast([P, U, TN]), ALU.is_equal))
                    st.settle()
                    v.sem_inc(oh_ready, 1)
                    v.tensor_tensor(sc[:, s, :, 0:2, :], oh[:, s].unsqueeze(2).to_broadcast([P, U, 2, TN]),
                                    stg[:, s, 0:2, :].rearrange("p k u -> p u k").unsqueeze(3).to_broadcast([P, U, 2, TN]),
                                    ALU.mult).then_inc(sv_ready, 1)

                def add(st, c, s):
                    for i in range(2):
                        j = v.value_load(g.gji[0:1, bass.ds(c * 2 + i, 1)], min_val=0, max_val=NT - 1)
                        v.wait_ge(summed, c * 2 + (2 * R + i + 1))
                        b = 4 * (s % 2) + 2 * i
                        a = g.acc[:, bass.ds(j, 1), :, :].rearrange("p o h w -> p (o h) w")
                        st(v.tensor_tensor(a, g.psum[0:TN, b:b + 2, 0:W], a, ALU.add))
                        st.settle()
                        v.sem_inc(bank_free, 1)

                v.memset(g.acc[:, :, :, :], 0.0).then_inc(own, 1)
                v.wait_ge(own, 1)
                K = 4
                st = Steps(v, own, 1)
                build(st, 0, 0)
                build(st, 1, 1)
                with v.Fori(0, NC // R - 1) as i:
                    for s in range(R):
                        c = i * R + s
                        st = Steps(v, own, c * K + 5)
                        build(st, c + 2, s % 2)
                        add(st, c, s)
                        assert st.n == K
                st = Steps(v, own, (NC - R) * K + 5)
                for c in range(NC - R, NC):
                    if c + 2 < NC:
                        build(st, c + 2, c % 2)
                    add(st, c, c % R)

            @block.tensor
            def _(pe):
                pe.sem_inc(summed, 2 * R)
                pe.sem_inc(bank_free, 4)
                with pe.Fori(0, NC // R) as i:
                    for s in range(R):
                        c = i * R + s
                        pe.wait_ge(sv_ready, c + 1)
                        pe.wait_ge(se_ready, c + 1)
                        pe.wait_ge(e_got[s], i * 16 + 16)
                        for u in range(U):
                            pe.wait_ge(got[s][u], i * 16 + 16)
                        for gi in range(2):
                            pe.wait_ge(bank_free, c * 2 + (gi + 1))
                            for h in range(2):
                                out = g.ps[4 * (s % 2) + 2 * gi + h]
                                for t in range(GT):
                                    u = GT * gi + t
                                    pe.matmul(out[0:TN, 0:D + 1], sc[:, s % 2, u, h, :], xr[:, s, u, 0:D + 1],
                                              start=t == 0, stop=t == GT - 1)
                                for t in range(GT):
                                    u = GT * gi + t
                                    last = pe.matmul(out[0:TN, D + 1:W], sc[:, s % 2, u, 2 + h, :], er[:, s, u, :],
                                                     start=t == 0, stop=t == GT - 1)
                            last.then_inc(summed, 1)


def key_softmax_context(nc, g, w, HB, name):
    F = HB * P
    with ExitStack() as ctx:
        sb, sem = alloc(nc, ctx)
        wkv = sb(f"{name}_wkv", [P, DB, 2 * F])
        wqt = sb(f"{name}_wqt", [P, HB, D])
        wout = sb(f"{name}_wout", [P, D]) if HB == 1 else None
        keys = sb(f"{name}_keys", [TN, NT, F])
        vals = sb(f"{name}_vals", [TN, NT, F])
        top5 = sb(f"{name}_top5", [TN, 5, F])
        top = sb(f"{name}_top", [TN, F])
        topc = sb(f"{name}_topc", [P, HB])
        topr = sb(f"{name}_topr", [TN, F])
        rsum = sb(f"{name}_rsum", [P, HB])
        cx = sb(f"{name}_cx", [P, HB, P])
        x1 = sb(f"{name}_x1", [P, D])
        loaded, formed, taken_a, own, top_ready, top_turned, topc_ready, topr_done = (
            sem(f"{name}_{x}") for x in ("loaded", "formed", "taken_a", "own", "top_ready", "top_turned",
                                         "topc_ready", "topr_done"))
        shifted, exped, summed, cx_ready, x1_done, x1_ready, mixed = (
            sem(f"{name}_{x}") for x in ("shifted", "exped", "summed", "cx_ready", "x1_done", "x1_ready", "mixed"))
        NL = 3 if HB == 1 else 2
        with nc.Block() as block:
            @block.sync
            def _(sp):
                sp.dma_start(wkv[:, :, :], w.kv).then_inc(loaded, 16)
                sp.dma_start(wqt[:, :, :], w.qt).then_inc(loaded, 16)
                if HB == 1:
                    sp.dma_start(wout[:, :], w.out).then_inc(loaded, 16)

            @block.tensor
            def _(pe):
                pe.wait_ge(loaded, 16 * NL)
                for j in range(NT):
                    if j >= 2:
                        pe.wait_ge(taken_a, 2 * (j - 1))
                    for k in range(DB):
                        last = pe.matmul(g.ps[j % 2][0:TN, 0:2 * F], g.XNT[:, k, j * TN:(j + 1) * TN], wkv[:, k, :],
                                         start=k == 0, stop=k == DB - 1)
                    last.then_inc(formed, 1)
                pe.wait_ge(top_ready, 1)
                for b in range(HB):
                    last = pe.transpose(g.ps[2][:, b * TN:(b + 1) * TN], top[:, b * P:(b + 1) * P], g.ident[0:TN, 0:TN])
                last.then_inc(top_turned, 1)
                pe.wait_ge(topc_ready, 1)
                for b in range(HB):
                    last = pe.transpose(g.ps[3][0:TN, b * P:(b + 1) * P], topc[:, b:b + 1].to_broadcast([P, TN]), g.ident[:, :])
                last.then_inc(topr_done, 1)
                for c in range(5):
                    pe.wait_ge(exped, c + 1)
                    for j in range(5 * c, 5 * c + 5):
                        for b in range(HB):
                            kk, vv = keys[:, j, b * P:(b + 1) * P], vals[:, j, b * P:(b + 1) * P]
                            l, r = (vv, kk) if HB == 1 else (kk, vv)
                            pe.matmul(g.ps[4 + b][:, 0:P], l, r, start=j == 0, stop=j == NT - 1)
                            last = pe.matmul(g.ps[6 + b][:, 0:1], kk, g.ones[0:TN, 0:1], start=j == 0, stop=j == NT - 1)
                last.then_inc(summed, 1)
                pe.wait_ge(cx_ready, 1)
                if HB == 1:
                    pe.matmul(g.ps[0][:, 0:D], cx[:, 0, :], wout[:, :], start=True, stop=True).then_inc(x1_done, 1)
                    pe.wait_ge(x1_ready, 1)
                for i in range(DB):
                    for b in range(HB):
                        rhs = x1[:, :] if HB == 1 else cx[:, b, :]
                        n = D if HB == 1 else P
                        last = pe.matmul(g.ps[1][:, i * D + b * P:i * D + b * P + n], wqt[:, b, i * P:(i + 1) * P], rhs,
                                         start=True, stop=True)
                last.then_inc(mixed, 1)

            @block.scalar
            def _(act):
                for j in range(NT):
                    act.wait_ge(formed, j + 1)
                    act.copy(keys[:, j, :], g.ps[j % 2][0:TN, 0:F]).then_inc(taken_a, 1)
                    act.copy(vals[:, j, :], g.ps[j % 2][0:TN, F:2 * F]).then_inc(taken_a, 1)
                for c in range(5):
                    act.wait_ge(shifted, c + 1)
                    act.activation(keys[:, 5 * c:5 * c + 5, :], keys[:, 5 * c:5 * c + 5, :], ACT.Exp).then_inc(exped, 1)

            @block.vector
            def _(v):
                st = Steps(v, own)
                for c in range(5):
                    v.wait_ge(taken_a, 10 * c + 10)
                    st(v.tensor_reduce(top5[:, c, :], keys[:, 5 * c:5 * c + 5, :].rearrange("p j f -> p f j"), AX.X, ALU.max))
                st.settle()
                st(v.tensor_reduce(top[:, :], top5[:, :, :].rearrange("p j f -> p f j"), AX.X, ALU.max))
                st.settle()
                v.sem_inc(top_ready, 1)
                v.wait_ge(top_turned, 1)
                for b in range(HB):
                    st(v.tensor_reduce(topc[:, b:b + 1], g.ps[2][:, b * TN:(b + 1) * TN], AX.X, ALU.max))
                st.settle()
                v.sem_inc(topc_ready, 1)
                v.wait_ge(topr_done, 1)
                st(v.tensor_copy(topr[:, :], g.ps[3][0:TN, 0:F]))
                st.settle()
                v.wait_ge(taken_a, 2 * NT)
                for c in range(5):
                    o = keys[:, 5 * c:5 * c + 5, :]
                    v.tensor_tensor(o, o, topr[:, :].unsqueeze(1).to_broadcast([TN, 5, F]), ALU.subtract).then_inc(shifted, 1)
                v.wait_ge(summed, 1)
                for b in range(HB):
                    st(v.tensor_scalar(rsum[:, b:b + 1], g.ps[6 + b][:, 0:1], w.inv_scale, None, ALU.mult))
                st.settle()
                st(v.reciprocal(rsum[:, :], rsum[:, :]))
                st.settle()
                for b in range(HB):
                    if HB == 1:
                        st(v.tensor_tensor(cx[:, b, :], g.ps[4 + b][:, 0:P], g.heads[:, :], ALU.mult))
                    else:
                        st(v.scalar_tensor_tensor(cx[:, b, :], g.ps[4 + b][:, 0:P], rsum[:, b:b + 1], g.heads[:, :], ALU.mult, ALU.mult))
                st.settle()
                v.sem_inc(cx_ready, 1)
                if HB == 1:
                    v.wait_ge(x1_done, 1)
                    v.tensor_scalar(x1[:, :], g.ps[0][:, 0:D], rsum[:, 0:1], None, ALU.mult).then_inc(x1_ready, 1)
                v.wait_ge(mixed, 1)
                st(v.tensor_copy(g.mix[:, :, :].rearrange("p i d -> p (i d)"), g.ps[1][:, 0:DB * D]))
                st.settle()


def move(nc, g, dst, src, name):
    with ExitStack() as ctx:
        moved = alloc(nc, ctx)[1](f"{name}_moved")
        with nc.Block() as block:
            @block.sync
            def _(sp):
                sp.dma_start(dst, src).then_inc(moved, 16)
                sp.wait_ge(moved, 16)


def combine0(nc, g):
    with ExitStack() as ctx:
        sb, sem = alloc(nc, ctx)
        rz = sb("c0_rz", [TN, NT, 2, 2])
        nst = sb("c0_nst", [TN, 2, 2, D + DE])
        nt = sb("c0_nt", [P, 2, 6, TN])
        bout = sb("c0_bout", [1, D])
        t2 = sb("c0_t2", [TN, 2, D])
        me = sb("c0_me", [TN, 2, D])
        ex = sb("c0_ex", [TN, 2, D])
        top = sb("c0_top", [TN, NT])
        tot = sb("c0_tot", [TN, NT])
        loaded, own, normed, turned, nt_v, nt_a, formed, t2_ready, top_ready, exped, banks_free, added = (
            sem(f"c0_{x}") for x in ("loaded", "own", "normed", "turned", "nt_v", "nt_a", "formed", "t2_ready",
                                     "top_ready", "exped", "banks_free", "added"))
        with nc.Block() as block:
            @block.sync
            def _(sp):
                sp.dma_start(bout[:, :], g.bout0).then_inc(loaded, 16)
                sp.dma_start(g.X[:, :, :], g.x.rearrange("(j p) d -> p j d", p=TN)).then_inc(loaded, 16)

            @block.tensor
            def _(pe):
                def turn_tile(j):
                    s = j % 2
                    pe.wait_ge(normed, j + 1)
                    if j >= 2:
                        pe.wait_ge(nt_v, j - 1)
                        pe.wait_ge(nt_a, j - 1)
                    for q in range(6):
                        last = pe.transpose(g.ps[4 * s + q // 3][:, (q % 3) * TN:(q % 3 + 1) * TN],
                                            nst[:, s, q // 3, (q % 3) * P:(q % 3 + 1) * P], g.ident[0:TN, 0:TN])
                    last.then_inc(turned, 1)

                def products(j):
                    s = j % 2
                    pe.wait_ge(nt_v, j + 1)
                    pe.wait_ge(nt_a, j + 1)
                    if j >= 2:
                        pe.wait_ge(banks_free, j - 1)
                    a, b = g.ps[4 * s + 2], g.ps[4 * s + 3]
                    for k in range(DB):
                        pe.matmul(b[0:TN, 0:D], g.XNT[:, k, j * TN:(j + 1) * TN], g.WC[:, k, :], start=k == 0, stop=False)
                    pe.matmul(b[0:TN, 0:D], g.ones[0:1, 0:TN], g.bc[:, :], start=False, stop=True)
                    for k in range(DB):
                        pe.matmul(b[0:TN, D:2 * D], g.XNT[:, k, j * TN:(j + 1) * TN], g.mix[:, k, :], start=k == 0, stop=False)
                    pe.matmul(b[0:TN, D:2 * D], g.ones[0:1, 0:TN], bout[:, :], start=False, stop=True)
                    for q in range(6):
                        h, k = q // 3, q % 3
                        rhs = g.Q[:, h, :] if k == 2 else g.G[:, h, k, :]
                        last = pe.matmul(a[0:TN, 0:D], nt[:, s, q, :], rhs, start=q == 0, stop=q == 5)
                    last.then_inc(formed, 1)

                pe.wait_ge(loaded, 32)
                turn_tile(0)
                for j in range(NT):
                    if j + 1 < NT:
                        turn_tile(j + 1)
                    products(j)

            @block.vector
            def _(v):
                st = Steps(v, own)
                z = g.acc[:, :, :, D:D + DE + 2:DE + 1]
                st(v.tensor_scalar(rz[:, :, :, :], z, 1e-30, None, ALU.max))
                st.settle()
                st(v.reciprocal(rz[:, :, :, :], rz[:, :, :, :]))
                st.settle()
                v.wait_ge(loaded, 32)

                def norm(j):
                    s = j % 2
                    if j >= 2:
                        v.wait_ge(turned, j - 1)
                    st(v.tensor_tensor(nst[:, s, :, 0:D], g.acc[:, j, :, 0:D],
                                       rz[:, j, :, 0:1].to_broadcast([TN, 2, D]), ALU.mult))
                    v.tensor_tensor(nst[:, s, :, D:D + DE], g.acc[:, j, :, D + 1:D + 1 + DE],
                                    rz[:, j, :, 1:2].to_broadcast([TN, 2, DE]), ALU.mult).then_inc(normed, 1)

                def take(j):
                    s = j % 2
                    v.wait_ge(turned, j + 1)
                    if j >= 2:
                        v.wait_ge(formed, j - 1)
                    v.tensor_copy(nt[:, s, 0:3, :].rearrange("p q n -> p (q n)"), g.ps[4 * s][:, 0:3 * TN]).then_inc(nt_v, 1)

                def join(j):
                    s = j % 2
                    v.wait_ge(t2_ready, j + 1)
                    st(v.tensor_tensor(me[:, s, :], g.ps[4 * s + 2][0:TN, 0:D], t2[:, s, :], ALU.add))
                    st.settle()
                    v.tensor_reduce(top[:, j:j + 1], me[:, s, :], AX.X, ALU.max, negate=True).then_inc(top_ready, 1)

                def add(j):
                    s = j % 2
                    v.wait_ge(exped, j + 1)
                    st(v.reciprocal(tot[:, j:j + 1], tot[:, j:j + 1]))
                    st(v.tensor_tensor(g.X[:, j, :], g.X[:, j, :], g.ps[4 * s + 3][0:TN, D:2 * D], ALU.add))
                    st.settle()
                    v.sem_inc(banks_free, 1)
                    v.scalar_tensor_tensor(g.X[:, j, :], ex[:, s, :], tot[:, j:j + 1], g.X[:, j, :], ALU.mult,
                                           ALU.add).then_inc(added, 1)

                norm(0)
                for j in range(NT + 2):
                    if j + 1 < NT:
                        norm(j + 1)
                    if j < NT:
                        take(j)
                    if j >= 2:
                        add(j - 2)
                    if 1 <= j <= NT:
                        join(j - 1)
                v.wait_ge(added, NT)

            @block.scalar
            def _(act):
                def take(j):
                    s = j % 2
                    act.wait_ge(turned, j + 1)
                    if j >= 2:
                        act.wait_ge(formed, j - 1)
                    act.copy(nt[:, s, 3:6, :].rearrange("p q n -> p (q n)"), g.ps[4 * s + 1][:, 0:3 * TN]).then_inc(nt_a, 1)

                def scale(j):
                    s = j % 2
                    act.wait_ge(formed, j + 1)
                    if j >= 2:
                        act.wait_ge(top_ready, j - 1)
                    act.activation(t2[:, s, :], g.ps[4 * s + 3][0:TN, 0:D], ACT.Copy, scale=g.deg[:, j:j + 1]).then_inc(t2_ready, 1)

                def exp(j):
                    s = j % 2
                    act.wait_ge(top_ready, j + 1)
                    if j >= 2:
                        act.wait_ge(added, j - 1)
                    act.activation(ex[:, s, :], me[:, s, :], ACT.Exp, bias=top[:, j:j + 1],
                                   accum_out=tot[:, j:j + 1]).then_inc(exped, 1)

                for j in range(NT + 2):
                    if j < NT:
                        take(j)
                    if j >= 2:
                        exp(j - 2)
                    if 1 <= j <= NT:
                        scale(j - 1)


def route0(nc, g):
    with ExitStack() as ctx:
        sb, sem = alloc(nc, ctx)
        mcol = sb("r0_mcol", [P, DB])
        wr = sb("r0_wr", [P, DB, XP])
        br = sb("r0_br", [1, XP])
        lg, rw, sc8, top8, w2 = (sb(f"r0_{x}", [1, XP]) for x in ("lg", "rw", "sc8", "top8", "w2"))
        one = sb("r0_one", [1, 8])
        idx = sb("r0_idx", [1, XP], U32)
        wb = sb("r0_wb", [P, 2])
        b2 = sb("r0_b2", [1, 2, D])
        loaded, own, m_ready, l_ready, ask, exped, idx_ready, w_ready, w_done, e_loaded = (
            sem(f"r0_{x}") for x in ("loaded", "own", "m_ready", "l_ready", "ask", "exped", "idx_ready", "w_ready",
                                     "w_done", "e_loaded"))
        with nc.Block() as block:
            @block.sync
            def _(sp):
                sp.dma_start(wr[:, :, :], g.wr0).then_inc(loaded, 16)
                sp.dma_start(br[:, :], g.br0).then_inc(loaded, 16)
                sp.wait_ge(idx_ready, 1)
                for i in range(2):
                    e = sp.value_load(idx[0:1, i:i + 1], min_val=0, max_val=XP - 1)
                    sp.dma_start(g.w1e[:, i, :, :], g.w1x0[bass.ds(e, 1)].rearrange("o p k f -> (o p) k f")).then_inc(e_loaded, 16)
                    sp.dma_start(g.w2e[:, i, :, :], g.w2x0[bass.ds(e, 1)].rearrange("o p k f -> (o p) k f")).then_inc(e_loaded, 16)
                    sp.dma_start(g.b1e[:, i, :], g.b1x0[bass.ds(e, 1)].rearrange("o p k -> (o p) k")).then_inc(e_loaded, 16)
                    sp.dma_start(b2[:, i, :], g.b2x0[bass.ds(e, 1)]).then_inc(e_loaded, 16)

            @block.tensor
            def _(pe):
                pe.wait_ge(loaded, 32)
                pe.wait_ge(m_ready, 1)
                for k in range(DB):
                    pe.matmul(g.ps[0][0:1, 0:XP], mcol[:, k:k + 1], wr[:, k, :], start=k == 0, stop=False)
                pe.matmul(g.ps[0][0:1, 0:XP], g.ones[0:1, 0:1], br[:, :], start=False, stop=True).then_inc(l_ready, 1)
                pe.wait_ge(w_ready, 1)
                pe.matmul(g.ps[1][:, 0:2], g.ones[0:1, :], w2[:, 0:2], start=True, stop=True).then_inc(w_done, 1)

            @block.scalar
            def _(act):
                act.wait_ge(ask, 1)
                act.activation(rw[:, :], lg[:, :], ACT.Exp, bias=one[:, 0:1], accum_out=one[:, 1:2]).then_inc(exped, 1)
                act.wait_ge(ask, 2)
                act.activation(sc8[:, :], rw[:, :], ACT.Exp, bias=one[:, 2:3], accum_out=one[:, 3:4]).then_inc(exped, 1)
                act.wait_ge(ask, 3)
                act.activation(w2[:, 0:2], top8[:, 0:2], ACT.Exp, bias=one[:, 4:5], accum_out=one[:, 5:6]).then_inc(exped, 1)

            @block.vector
            def _(v):
                st = Steps(v, own)

                def do(ins):
                    st(ins)
                    st.settle()

                do(v.tensor_reduce(mcol[:, :], g.XNT[:, :, :], AX.X, ALU.add))
                do(v.tensor_scalar(mcol[:, :], mcol[:, :], 1.0 / N, None, ALU.mult))
                v.sem_inc(m_ready, 1)
                v.wait_ge(l_ready, 1)
                do(v.tensor_copy(lg[:, :], g.ps[0][0:1, 0:XP]))
                do(v.tensor_reduce(one[:, 0:1], lg[:, :], AX.X, ALU.max, negate=True))
                v.sem_inc(ask, 1)
                v.wait_ge(exped, 1)
                do(v.reciprocal(one[:, 1:2], one[:, 1:2]))
                do(v.tensor_scalar(rw[:, :], rw[:, :], one[:, 1:2], None, ALU.mult))
                do(v.tensor_scalar(sc8[:, :], rw[:, :], float(N), 1e-20, ALU.mult, ALU.max))
                do(v.reciprocal(sc8[:, :], sc8[:, :]))
                do(v.tensor_scalar(sc8[:, :], sc8[:, :], float(CAP), 1.0, ALU.mult, ALU.min))
                do(v.tensor_tensor(rw[:, :], rw[:, :], sc8[:, :], ALU.mult))
                do(v.tensor_reduce(one[:, 2:3], rw[:, :], AX.X, ALU.max, negate=True))
                v.sem_inc(ask, 1)
                v.wait_ge(exped, 2)
                do(v.reciprocal(one[:, 3:4], one[:, 3:4]))
                do(v.tensor_scalar(rw[:, :], sc8[:, :], one[:, 3:4], None, ALU.mult))
                do(v.max(top8[:, :], rw[:, :]))
                do(v.max_index(idx[:, :], top8[:, :], rw[:, :]))
                v.sem_inc(idx_ready, 1)
                do(v.tensor_scalar(one[:, 4:5], top8[:, 0:1], -1.0, None, ALU.mult))
                v.sem_inc(ask, 1)
                v.wait_ge(exped, 3)
                do(v.reciprocal(one[:, 5:6], one[:, 5:6]))
                do(v.tensor_scalar(w2[:, 0:2], w2[:, 0:2], one[:, 5:6], None, ALU.mult))
                v.sem_inc(w_ready, 1)
                v.wait_ge(w_done, 1)
                do(v.tensor_copy(wb[:, :], g.ps[1][:, 0:2]))
                v.wait_ge(e_loaded, 16 * 8)
                for i in range(2):
                    st(v.tensor_scalar(g.w2e[:, i, :, :], g.w2e[:, i, :, :], wb[:, i:i + 1], None, ALU.mult))
                do(v.tensor_scalar(g.b2e[:, :], b2[:, 0, :], w2[:, 0:1], None, ALU.mult))
                do(v.scalar_tensor_tensor(g.b2e[:, :], b2[:, 1, :], w2[:, 1:2], g.b2e[:, :], ALU.mult, ALU.add))


def experts0(nc, g):
    Q = 4
    FB = F0 // P
    NI = 2 * FB
    CW = Q * TN
    with ExitStack() as ctx:
        sb, sem = alloc(nc, ctx)
        ht = sb("x0_ht", [P, 2, NI, CW])
        formed, taken, y_formed, y_taken, ht_free = (sem(f"x0_{x}") for x in ("formed", "taken", "y_formed", "y_taken", "ht_free"))
        NCK = NT // Q
        with nc.Block() as block:
            @block.tensor
            def _(pe):
                pe.sem_inc(taken, 4)
                pe.sem_inc(y_taken, 4)

                def first(c, s, w=CW):
                    for i in range(NI):
                        pe.wait_ge(taken, c * NI + (i + 1))
                        for k in range(DB):
                            last = pe.matmul(g.ps[i % 4][:, 0:w], g.w1e[:, i // FB, k, (i % FB) * P:(i % FB + 1) * P],
                                             g.XNT[:, k, bass.ds(c * CW, w)], start=k == 0, stop=k == DB - 1)
                        last.then_inc(formed, 1)

                def second(c, s, q=Q):
                    pe.wait_ge(taken, c * NI + (NI + 4))
                    for t in range(q):
                        pe.wait_ge(y_taken, c * Q + (t + 1))
                        for i in range(NI):
                            pe.matmul(g.ps[4 + t][0:TN, 0:D], ht[:, s, i, t * TN:(t + 1) * TN], g.w2e[:, i // FB, i % FB, :],
                                      start=i == 0, stop=False)
                        last = pe.matmul(g.ps[4 + t][0:TN, 0:D], g.ones[0:1, 0:TN], g.b2e[:, :], start=False, stop=True)
                        last.then_inc(y_formed, 1)

                first(0, 0)
                with pe.Fori(0, (NCK - 1) // 2) as i:
                    for s in range(2):
                        c = i * 2 + 1 + s
                        first(c, 1 - s)
                        second(c - 1, s)
                assert NCK % 2 == 0
                first(NCK - 1, 1)
                second(NCK - 2, 0)
                first(NCK, 0, (NT - Q * NCK) * TN)
                second(NCK - 1, 1)
                second(NCK, 0, NT - Q * NCK)

            @block.scalar
            def _(act):
                def take(c, s, w=CW):
                    for i in range(NI):
                        act.wait_ge(formed, c * NI + (i + 1))
                        if i == 0:
                            act.wait_ge(ht_free, c + 1)
                        act.activation(ht[:, s, i, 0:w], g.ps[i % 4][:, 0:w], ACT.Gelu,
                                       bias=g.b1e[:, i // FB, i % FB:i % FB + 1]).then_inc(taken, 1)

                with act.Fori(0, NCK // 2) as i:
                    for s in range(2):
                        take(i * 2 + s, s)
                take(NCK, 0, (NT - Q * NCK) * TN)

            @block.vector
            def _(v):
                v.sem_inc(ht_free, 2)

                def add(c, q=Q):
                    for t in range(q):
                        v.wait_ge(y_formed, c * Q + (t + 1))
                        o = g.XN[:, bass.ds(c * Q + t, 1), 0:D].rearrange("p o d -> p (o d)")
                        v.tensor_tensor(o, g.ps[4 + t][0:TN, 0:D], o, ALU.add).then_inc(y_taken, 1)
                    v.sem_inc(ht_free, 1)

                with v.Fori(0, NCK) as c:
                    add(c)
                add(NCK, NT - Q * NCK)
                v.wait_ge(y_taken, NT + 4)


def scaled_residual(nc, g):
    with ExitStack() as ctx:
        sb, sem = alloc(nc, ctx)
        gb = sb("sr_gb", [TN, 2, D])
        loaded, own = sem("sr_loaded"), sem("sr_own")
        with nc.Block() as block:
            @block.sync
            def _(sp):
                sp.dma_start(gb[:, :, :], g.gb0.to_broadcast([TN, 2, D])).then_inc(loaded, 16)

            @block.vector
            def _(v):
                st = Steps(v, own)
                v.wait_ge(loaded, 16)
                xn = g.XN[:, :, 0:D]
                st(v.tensor_tensor(xn, xn, gb[:, 0:1, :].to_broadcast([TN, NT, D]), ALU.mult))
                st(v.tensor_tensor(g.X[:, :, :], g.X[:, :, :], gb[:, 1:2, :].to_broadcast([TN, NT, D]), ALU.add))
                st.settle()
                st(v.tensor_tensor(g.X[:, :, :], g.X[:, :, :], xn, ALU.add))
                st.settle()


def hidden1(nc, g):
    with ExitStack() as ctx:
        sb, sem = alloc(nc, ctx)
        w = sb("h1_w", [P, DB, HROW])
        ab = sb("h1_ab", [P, 2, D])
        prod = sb("h1_prod", [P, DB, 2, D])
        low = sb("h1_low", [TN, 2, HROW])
        loaded, own, w_ready, formed, taken, stored = (sem(f"h1_{x}") for x in ("loaded", "own", "w_ready", "formed", "taken", "stored"))
        with nc.Block() as block:
            @block.sync
            def _(sp):
                sp.dma_start(w[:, :, 0:D], g.w1h).then_inc(loaded, 16)
                sp.dma_start(ab[:, :, :], g.a1h.to_broadcast([P, 2, D])).then_inc(loaded, 16)
                sp.wait_ge(taken, NT)
                sp.dma_start(g.hd.rearrange("(j p) c -> p j c", p=TN), g.H[:, :, :]).then_inc(stored, 16)
                sp.wait_ge(stored, 16)

            @block.vector
            def _(v):
                st = Steps(v, own)
                v.wait_ge(loaded, 32)
                for k in range(DB):
                    st(v.tensor_tensor(prod[:, k], w[:, k, 0:D].unsqueeze(1).to_broadcast([P, 2, D]), ab[:, :, :], ALU.mult))
                st.settle()
                for k in range(DB):
                    st(v.tensor_reduce(w[:, k, D:D + 8].rearrange("p (c h) -> p c h", c=2),
                                       prod[:, k].rearrange("p c (h o) -> p c h o", h=4), AX.X, ALU.add))
                st.settle()
                v.sem_inc(w_ready, 1)
                for j in range(NT):
                    v.wait_ge(formed, j + 1)
                    st(v.tensor_scalar(low[:, j % 2, :], g.ps[j % 2][0:TN, 0:HROW], 0.0, None, ALU.min))
                    st.settle()
                    v.scalar_tensor_tensor(g.H[:, j, :], g.ps[j % 2][0:TN, 0:HROW], 0.0, low[:, j % 2, :], ALU.max,
                                           ALU.add).then_inc(taken, 1)
                v.wait_ge(taken, NT)

            @block.tensor
            def _(pe):
                pe.wait_ge(w_ready, 1)
                for j in range(NT):
                    if j >= 2:
                        pe.wait_ge(taken, j - 1)
                    for k in range(DB):
                        last = pe.matmul(g.ps[j % 2][0:TN, 0:HROW], g.XNT[:, k, j * TN:(j + 1) * TN], w[:, k, :],
                                         start=k == 0, stop=k == DB - 1)
                    last.then_inc(formed, 1)


def gather_sums1(nc, g):
    U = 4
    NC = ST // U
    R = 4
    W = D + 4
    with ExitStack() as ctx:
        sb, sem = alloc(nc, ctx)
        idx = sb("a1_idx", [P, R, U], I32)
        hr = sb("a1_hr", [P, R, U, HROW])
        oh = sb("a1_oh", [P, R, U, TN])
        oht = sb("a1_oht", [TN, 2, U, P])
        s4 = sb("a1_s4", [P, 2, U, 4])
        idx_ready, gate, agate, own, oh_ready, turned, oht_ready, looked, s_ready, e_ready, rows_ready, summed, \
            bank_free = (
                sem(f"a1_{x}") for x in ("idx_ready", "gate", "agate", "own", "oh_ready", "turned", "oht_ready",
                                         "looked", "s_ready", "e_ready", "rows_ready", "summed", "bank_free"))
        got = [[sem(f"a1_got{s}_{u}") for u in range(U)] for s in range(R)]
        with nc.Block() as block:
            @block.gpsimd
            def _(pool):
                with pool.Fori(0, NC // R) as i:
                    for s in range(R):
                        pool.wait_ge(idx_ready, i * R + (s + 1))
                        pool.sem_inc(gate, 1)
                        for u in range(U):
                            pool.indirect_dma_start(hr[:, s, u, :], None, g.hd, bass.IndirectOffsetOnAxis(
                                ap=idx[:, s, u:u + 1], axis=0)).then_inc(got[s][u], 16)

            @block.scalar
            def _(act):
                def put(c, s):
                    act.wait_ge(summed, c * 2 + 2)
                    act.sem_inc(agate, 1)
                    act.copy(idx[:, s], g.sdst[:, bass.ds(c * U, U)]).then_inc(idx_ready, 1)

                def turn_take(c, s):
                    act.wait_ge(turned, c + 1)
                    act.copy(oht[:, s].rearrange("p u e -> p (u e)"), g.ps[s][0:TN, :]).then_inc(oht_ready, 1)

                def weight(c, s):
                    act.wait_ge(s_ready, c + 1)
                    act.activation(hr[:, s, :, D:D + 4], s4[:, s % 2], ACT.Exp, scale=-1.0).then_inc(e_ready, 1)

                for c in range(3):
                    put(c, c)
                turn_take(0, 0)
                weight(0, 0)
                turn_take(1, 1)
                with act.Fori(0, NC // R - 1) as i:
                    for s in range(R):
                        c = i * R + s
                        put(c + 3, (s + 3) % R)
                        turn_take(c + 2, s % 2)
                        weight(c + 1, (s + 1) % R)
                for c in range(NC - R, NC):
                    if c + 2 < NC:
                        turn_take(c + 2, c % 2)
                    if c + 1 < NC:
                        weight(c + 1, (c + 1) % R)
                    if c + 3 < NC:
                        put(c + 3, (c + 3) % R)

            @block.vector
            def _(v):
                def build(c, s):
                    v.wait_ge(summed, c * 2 + 2)
                    v.tensor_tensor(oh[:, s], g.iota[:, 0:TN].unsqueeze(1).to_broadcast([P, U, TN]),
                                    g.sw[:, 4, bass.ds(c * U, U)].unsqueeze(2).to_broadcast([P, U, TN]),
                                    ALU.is_equal).then_inc(oh_ready, 1)

                def score(st, c, s, uses):
                    v.wait_ge(looked, c + 1)
                    for u in range(U):
                        v.wait_ge(got[s][u], uses * 16)
                    st(v.tensor_tensor(s4[:, s % 2], g.ps[2 + s % 2][:, 0:4 * U].rearrange("p (u h) -> p u h", u=U),
                                       hr[:, s, :, D:D + 4], ALU.add))
                    st.settle()
                    v.scalar_tensor_tensor(s4[:, s % 2], s4[:, s % 2], 0.2, s4[:, s % 2], ALU.mult, ALU.max)\
                        .then_inc(s_ready, 1)

                def weigh(st, c, s):
                    v.wait_ge(e_ready, c + 1)
                    st(v.tensor_scalar(hr[:, s, :, D:D + 4], hr[:, s, :, D:D + 4], 0.0, None, ALU.max))
                    st.settle()
                    h = hr[:, s, :, 0:D].rearrange("p u (h o) -> p u h o", h=4)
                    v.tensor_tensor(h, h, hr[:, s, :, D:D + 4].unsqueeze(3).to_broadcast([P, U, 4, D // 4]),
                                    ALU.mult).then_inc(rows_ready, 1)

                def add(st, c, s):
                    for i in range(2):
                        j = v.value_load(g.gji[0:1, bass.ds(c * 2 + i, 1)], min_val=0, max_val=NT - 1)
                        v.wait_ge(summed, c * 2 + (2 * R + i + 1))
                        a = g.acc1[:, bass.ds(j, 1), :].rearrange("p o w -> p (o w)")
                        st(v.tensor_tensor(a, g.ps[4 + 2 * (s % 2) + i][0:TN, 0:W], a, ALU.add))
                        st.settle()
                        v.sem_inc(bank_free, 1)

                v.memset(g.acc1[:, :, :], 0.0).then_inc(own, 1)
                v.wait_ge(own, 1)
                K = 4
                st = Steps(v, own, 1)
                for c in range(3):
                    build(c, c)
                score(st, 0, 0, 1)
                weigh(st, 0, 0)
                score(st, 1, 1, 1)
                build(3, 3)
                weigh(st, 1, 1)
                with v.Fori(0, NC // R - 1) as i:
                    for s in range(R):
                        c = i * R + s
                        st = Steps(v, own, c * K + 5)
                        score(st, c + 2, (s + 2) % R, i + (1 if s < R - 2 else 2))
                        build(c + 4, s)
                        add(st, c, s)
                        weigh(st, c + 2, (s + 2) % R)
                        assert st.n == K
                st = Steps(v, own, (NC - R) * K + 5)
                for c in range(NC - R, NC):
                    if c + 2 < NC:
                        score(st, c + 2, (c + 2) % R, (c + 2) // R + 1)
                    add(st, c, c % R)
                    if c + 2 < NC:
                        weigh(st, c + 2, (c + 2) % R)

            @block.tensor
            def _(pe):
                pe.sem_inc(summed, 2 * R)
                pe.sem_inc(bank_free, 4)

                def turn_one_hot(c, s):
                    pe.wait_ge(oh_ready, c + 1)
                    for u in range(U):
                        last = pe.transpose(g.ps[s % 2][0:TN, u * P:(u + 1) * P], oh[:, s, u, :], g.ident[:, :])
                    last.then_inc(turned, 1)

                def look(c, s):
                    pe.wait_ge(oht_ready, c + 1)
                    for i in range(2):
                        j = pe.value_load(g.gji[0:1, bass.ds(c * 2 + i, 1)], min_val=0, max_val=NT - 1)
                        for t in range(GT):
                            u = GT * i + t
                            last = pe.matmul(g.ps[2 + s % 2][:, 4 * u:4 * u + 4], oht[:, s % 2, u, :],
                                             g.H[:, bass.ds(j, 1), D + 4:D + 8].rearrange("p o h -> p (o h)"),
                                             start=True, stop=True)
                    last.then_inc(looked, 1)

                def sums(c, s):
                    pe.wait_ge(rows_ready, c + 1)
                    for i in range(2):
                        pe.wait_ge(bank_free, c * 2 + (i + 1))
                        for t in range(GT):
                            u = GT * i + t
                            last = pe.matmul(g.ps[4 + 2 * (s % 2) + i][0:TN, 0:W], oh[:, s, u, :], hr[:, s, u, 0:W],
                                             start=t == 0, stop=t == GT - 1)
                        last.then_inc(summed, 1)

                turn_one_hot(0, 0)
                look(0, 0)
                turn_one_hot(1, 1)
                look(1, 1)
                with pe.Fori(0, NC // R - 1) as i:
                    for s in range(R):
                        c = i * R + s
                        turn_one_hot(c + 2, (s + 2) % R)
                        sums(c, s)
                        look(c + 2, (s + 2) % R)
                for c in range(NC - R, NC):
                    if c + 2 < NC:
                        turn_one_hot(c + 2, (c + 2) % R)
                    sums(c, c % R)
                    if c + 2 < NC:
                        look(c + 2, (c + 2) % R)


def combine1(nc, g):
    K = 5
    with ExitStack() as ctx:
        sb, sem = alloc(nc, ctx)
        rz = sb("c1_rz", [TN, NT, 4])
        lowr = sb("c1_lowr", [TN, 2, K, D])
        own, low_ready, exped = sem("c1_own"), sem("c1_low_ready"), sem("c1_exped")
        with nc.Block() as block:
            @block.vector
            def _(v):
                st = Steps(v, own)

                def do(ins):
                    st(ins)
                    st.settle()

                do(v.tensor_scalar(rz[:, :, :], g.acc1[:, :, D:D + 4], 1e-37, None, ALU.max))
                do(v.reciprocal(rz[:, :, :], rz[:, :, :]))
                for c in range(NT // K):
                    s = slice(K * c, K * c + K)
                    a = g.acc1[:, s, 0:D]
                    x = g.X[:, s, :]
                    low = lowr[:, c % 2]
                    do(v.tensor_scalar(low, a, 0.0, None, ALU.min))
                    for jj in range(K * c, K * c + K):
                        st(v.scalar_tensor_tensor(g.acc1[:, jj, 0:D], g.acc1[:, jj, 0:D], 0.0, lowr[:, c % 2, jj - K * c, :],
                                                  ALU.max, ALU.add))
                    st.settle()
                    for jj in range(K * c, K * c + K):
                        aj = g.acc1[:, jj, 0:D].rearrange("p (h o) -> p h o", h=4)
                        st(v.tensor_tensor(aj, aj, rz[:, jj, :].unsqueeze(2).to_broadcast([TN, 4, D // 4]), ALU.mult))
                    st.settle()
                    do(v.tensor_scalar(low, a, 0.0, None, ALU.min))
                    v.sem_inc(low_ready, 1)
                    v.wait_ge(exped, 2 * c + 1)
                    do(v.scalar_tensor_tensor(a, a, 0.0, low, ALU.max, ALU.add))
                    do(v.tensor_scalar(low, a, 1.0, 0.0, ALU.subtract, ALU.min))
                    v.sem_inc(low_ready, 1)
                    v.wait_ge(exped, 2 * c + 2)
                    do(v.scalar_tensor_tensor(a, a, 1.0, low, ALU.max, ALU.add))
                    do(v.scalar_tensor_tensor(x, a, 2.0, x, ALU.subtract, ALU.add))

            @block.scalar
            def _(act):
                for c in range(NT // K):
                    for r in range(2):
                        act.wait_ge(low_ready, 2 * c + r + 1)
                        act.activation(lowr[:, c % 2], lowr[:, c % 2], ACT.Exp).then_inc(exped, 1)


def gate_weights(nc, g):
    with ExitStack() as ctx:
        loaded = alloc(nc, ctx)[1]("gw_loaded")
        with nc.Block() as block:
            @block.sync
            def _(sp):
                for t, f in ((g.wg1t[:, :, :], g.wg1), (g.wg2t[:, :], g.wg2), (g.wprojt[:, :, :], g.wproj),
                             (g.gcols[:, :], g.gcols1), (g.bg1t[:, :], g.bg1), (g.bprojt[:, :], g.bproj)):
                    sp.dma_start(t, f).then_inc(loaded, 16)
                sp.wait_ge(loaded, 16 * 6)


def gated_mix(nc, g):
    Q = 4
    CW = Q * TN
    GH = D // 4
    NCK = NT // Q
    with ExitStack() as ctx:
        sb, sem = alloc(nc, ctx)
        hg = sb("gm_hg", [GH, 2, CW])
        gt = sb("gm_gt", [P, DB, CW])
        og = sb("gm_og", [P, 2, DB, CW])
        hid_formed, hg_ready, gate_formed, gt_ready, gt_free, out_formed, og_ready, y_formed, y_taken = (
            sem(f"gm_{x}") for x in ("hid_formed", "hg_ready", "gate_formed", "gt_ready", "gt_free", "out_formed",
                                     "og_ready", "y_formed", "y_taken"))
        with nc.Block() as block:
            @block.tensor
            def _(pe):
                def hid(c, s, w=CW):
                    for k in range(DB):
                        last = pe.matmul(g.ps[s][0:GH, 0:w], g.wg1t[:, k, :], g.XGT[:, k, bass.ds(c * CW, w)],
                                         start=k == 0, stop=k == DB - 1)
                    last.then_inc(hid_formed, 1)

                def gates(c, s, w=CW):
                    pe.wait_ge(hg_ready, c + 1)
                    pe.wait_ge(gt_free, c + 1)
                    for b in range(DB):
                        pe.matmul(g.ps[2 + b][:, 0:w], g.wg2t[:, b * P:(b + 1) * P], hg[:, s, 0:w],
                                  start=True, stop=True).then_inc(gate_formed, 1)
                    for b in range(DB):
                        for k in range(DB):
                            last = pe.matmul(g.ps[4 + b][:, 0:w], g.mix[:, k, b * P:(b + 1) * P],
                                             g.XNT[:, k, bass.ds(c * CW, w)], start=k == 0, stop=k == DB - 1)
                        last.then_inc(out_formed, 1)

                def project(c, s, q=Q):
                    pe.wait_ge(og_ready, c * 2 + 2)
                    for t in range(q):
                        pe.wait_ge(y_taken, c * Q + (t + 1))
                        for b in range(DB):
                            pe.matmul(g.ps[6 + t % 2][0:TN, 0:D], og[:, s, b, t * TN:(t + 1) * TN], g.wprojt[:, b, :],
                                      start=b == 0, stop=False)
                        pe.matmul(g.ps[6 + t % 2][0:TN, 0:D], g.ones[0:1, 0:TN], g.bprojt[:, :], start=False,
                                  stop=True).then_inc(y_formed, 1)

                pe.sem_inc(y_taken, 2)
                hid(0, 0)
                hid(1, 1)
                gates(0, 0)
                with pe.Fori(0, (NCK - 2) // 2) as i:
                    for s in range(2):
                        c = i * 2 + s
                        hid(c + 2, s)
                        gates(c + 1, 1 - s)
                        project(c, s)
                assert NCK % 2 == 0
                w = (NT - Q * NCK) * TN
                hid(NCK, 0, w)
                gates(NCK - 1, 1)
                project(NCK - 2, 0)
                gates(NCK, 0, w)
                project(NCK - 1, 1)
                project(NCK, 0, NT - Q * NCK)

            @block.scalar
            def _(act):
                def hidden(c, s, w=CW):
                    act.wait_ge(hid_formed, c + 1)
                    act.activation(hg[:, s, 0:w], g.ps[s][0:GH, 0:w], ACT.Gelu, bias=g.bg1t[:, :]).then_inc(hg_ready, 1)

                def gate(c, w=CW):
                    act.wait_ge(gt_free, c + 1)
                    for b in range(DB):
                        act.wait_ge(gate_formed, c * 2 + (b + 1))
                        act.activation(gt[:, b, 0:w], g.ps[2 + b][:, 0:w], ACT.Sigmoid,
                                       bias=g.gcols[:, 4 + b:5 + b]).then_inc(gt_ready, 1)

                w = (NT - Q * NCK) * TN
                hidden(0, 0)
                with act.Fori(0, NCK // 2 - 1) as i:
                    for s in range(2):
                        c = i * 2 + s
                        hidden(c + 1, 1 - s)
                        gate(c)
                hidden(NCK - 1, 1)
                gate(NCK - 2)
                hidden(NCK, 0, w)
                gate(NCK - 1)
                gate(NCK, w)

            @block.vector
            def _(v):
                def product(c, s, w=CW):
                    for b in range(DB):
                        v.wait_ge(gt_ready, c * 2 + (b + 1))
                        v.wait_ge(out_formed, c * 2 + (b + 1))
                        v.tensor_tensor(og[:, s, b, 0:w], g.ps[4 + b][:, 0:w], gt[:, b, 0:w], ALU.mult).then_inc(og_ready, 1)
                    v.wait_ge(og_ready, c * 2 + 2)
                    v.sem_inc(gt_free, 1)

                def add(c, q=Q):
                    for t in range(q):
                        v.wait_ge(y_formed, c * Q + (t + 1))
                        o = g.X[:, bass.ds(c * Q + t, 1), :].rearrange("p o d -> p (o d)")
                        v.tensor_tensor(o, g.ps[6 + t % 2][0:TN, 0:D], o, ALU.add).then_inc(y_taken, 1)

                v.sem_inc(gt_free, 1)
                product(0, 0)
                with v.Fori(0, NCK // 2 - 1) as i:
                    for s in range(2):
                        c = i * 2 + s
                        product(c + 1, 1 - s)
                        add(c)
                product(NCK - 1, 1)
                add(NCK - 2)
                product(NCK, 0, (NT - Q * NCK) * TN)
                add(NCK - 1)
                add(NCK, NT - Q * NCK)
                v.wait_ge(y_taken, NT + 2)


def route1(nc, g):
    with ExitStack() as ctx:
        sb, sem = alloc(nc, ctx)
        gw = sb("r1_gw", [P, DB, XP])
        gb = sb("r1_gb", [1, XP])
        lg, oh, at, cum, tot = (sb(f"r1_{x}", [TN, NT, XP]) for x in ("lg", "oh", "at", "cum", "tot"))
        left = sb("r1_left", [TN, XP])
        top, esum, best, pos, kept, row = (sb(f"r1_{x}", [TN, NT]) for x in ("top", "esum", "best", "pos", "kept", "row"))
        goal = sb("r1_goal", [TN, NT], I32)
        loaded, own, formed, shifted, exped, ranked, counted, left_ready, goal_ready, sent = (
            sem(f"r1_{x}") for x in ("loaded", "own", "formed", "shifted", "exped", "ranked", "counted", "left_ready",
                                     "goal_ready", "sent"))
        with nc.Block() as block:
            @block.sync
            def _(sp):
                sp.dma_start(gw[:, :, :], g.gatew).then_inc(loaded, 16)
                sp.dma_start(gb[:, :], g.gateb).then_inc(loaded, 16)

            @block.tensor
            def _(pe):
                pe.wait_ge(loaded, 32)
                for j in range(NT):
                    o = g.ps[0][0:TN, j * XP:(j + 1) * XP]
                    for k in range(DB):
                        pe.matmul(o, g.XNT[:, k, j * TN:(j + 1) * TN], gw[:, k, :], start=k == 0, stop=False)
                    last = pe.matmul(o, g.ones[0:1, 0:TN], gb[:, :], start=False, stop=True)
                last.then_inc(formed, 1)
                pe.wait_ge(ranked, 1)
                f = oh[:, :, :].rearrange("p j e -> p (j e)")
                pe.matmul(g.ps[1][0:TN, 0:NT * XP], g.after[0:TN, 0:TN], f, start=True, stop=True).then_inc(counted, 1)
                pe.matmul(g.ps[2][0:TN, 0:NT * XP], g.ones[0:TN, 0:TN], f, start=True, stop=True).then_inc(counted, 1)

            @block.scalar
            def _(act):
                act.wait_ge(shifted, 1)
                act.activation(lg[:, :, :], lg[:, :, :], ACT.Exp).then_inc(exped, 1)

            @block.gpsimd
            def _(pool):
                pool.iota(left[:, :], [[-1, XP]], base=XP, channel_multiplier=0,
                          allow_small_or_imprecise_dtypes=True).then_inc(left_ready, 1)
                pool.wait_ge(goal_ready, 1)
                for j in range(NT):
                    pool.indirect_dma_start(g.xbuf, bass.IndirectOffsetOnAxis(ap=goal[:, j:j + 1], axis=0),
                                            g.XN[:, j, 0:D], None, bounds_check=XP * CAP - 1,
                                            oob_is_err=False).then_inc(sent, 16)
                pool.wait_ge(sent, 16 * NT)

            @block.vector
            def _(v):
                st = Steps(v, own)

                def do(ins):
                    st(ins)
                    st.settle()

                def wide(t):
                    return t.unsqueeze(2).to_broadcast([TN, NT, XP])

                v.wait_ge(formed, 1)
                do(v.tensor_copy(lg[:, :, :].rearrange("p j e -> p (j e)"), g.ps[0][0:TN, 0:NT * XP]))
                do(v.tensor_reduce(top[:, :], lg[:, :, :], AX.X, ALU.max))
                do(v.tensor_tensor(lg[:, :, :], lg[:, :, :], wide(top[:, :]), ALU.subtract))
                v.sem_inc(shifted, 1)
                v.wait_ge(exped, 1)
                do(v.tensor_reduce(top[:, :], lg[:, :, :], AX.X, ALU.max))
                do(v.tensor_reduce(esum[:, :], lg[:, :, :], AX.X, ALU.add))
                do(v.reciprocal(esum[:, :], esum[:, :]))
                do(v.tensor_tensor(g.share[:, :], top[:, :], esum[:, :], ALU.mult))
                do(v.tensor_tensor(oh[:, :, :], lg[:, :, :], wide(top[:, :]), ALU.is_equal))
                v.wait_ge(left_ready, 1)
                lb = left[:, :].unsqueeze(1).to_broadcast([TN, NT, XP])
                do(v.tensor_tensor(at[:, :, :], oh[:, :, :], lb, ALU.mult))
                do(v.tensor_reduce(best[:, :], at[:, :, :], AX.X, ALU.max))
                do(v.tensor_scalar(best[:, :], best[:, :], 1.0, None, ALU.max))
                do(v.tensor_tensor(oh[:, :, :], lb, wide(best[:, :]), ALU.is_equal))
                v.sem_inc(ranked, 1)
                v.wait_ge(counted, 2)
                do(v.tensor_copy(tot[:, :, :].rearrange("p j e -> p (j e)"), g.ps[2][0:TN, 0:NT * XP]))
                for e in range(XP):
                    st(v.tensor_tensor_scan(cum[:, :, e], tot[:, :, e], tot[:, :, e], 0.0, ALU.add, ALU.bypass))
                st.settle()
                do(v.tensor_tensor(cum[:, :, :], cum[:, :, :], tot[:, :, :], ALU.subtract))
                do(v.tensor_tensor(cum[:, :, :], g.ps[1][0:TN, 0:NT * XP].rearrange("p (j e) -> p j e", e=XP), cum[:, :, :],
                                   ALU.add))
                do(v.tensor_tensor(cum[:, :, :], cum[:, :, :], oh[:, :, :], ALU.mult))
                do(v.tensor_reduce(pos[:, :], cum[:, :, :], AX.X, ALU.add))
                do(v.tensor_scalar(kept[:, :], pos[:, :], float(CAP), None, ALU.is_lt))
                do(v.tensor_tensor(g.share[:, :], g.share[:, :], kept[:, :], ALU.mult))
                do(v.tensor_scalar(best[:, :], best[:, :], -float(CAP), float(XP * CAP), ALU.mult, ALU.add))
                do(v.tensor_scalar(row[:, :], pos[:, :], float(CAP - 1), None, ALU.min))
                do(v.tensor_tensor(g.home[:, :], row[:, :], best[:, :], ALU.add))
                do(v.tensor_tensor(row[:, :], pos[:, :], best[:, :], ALU.add))
                do(v.tensor_scalar(kept[:, :], kept[:, :], -float(XP * CAP), float(XP * CAP), ALU.mult, ALU.add))
                do(v.tensor_tensor(goal[:, :], row[:, :], kept[:, :], ALU.add))
                v.sem_inc(goal_ready, 1)


def experts1(nc, g):
    FB = F1 // P
    RT = -(-CAP // P)
    LR = CAP - (RT - 1) * P
    with ExitStack() as ctx:
        sb, sem = alloc(nc, ctx)
        w1 = sb("x1_w1", [P, 2, DB, F1])
        w2 = sb("x1_w2", [P, 2, FB, D])
        b1 = sb("x1_b1", [P, 2, FB])
        b2 = sb("x1_b2", [P, XP, D])
        xb = sb("x1_xb", [P, 2, RT, D])
        xt = sb("x1_xt", [P, 2, DB, CAP])
        ht = sb("x1_ht", [P, FB, CAP])
        yb = sb("x1_yb", [P, 2, RT, D])
        b2_got, turned, xt_ready, rows_free, formed, taken, y_formed, y_taken, w_free, y_free = (
            sem(f"x1_{x}") for x in ("b2_got", "turned", "xt_ready", "rows_free", "formed", "taken", "y_formed", "y_taken",
                                     "w_free", "y_free"))
        w_got, x_got, stored = ([sem(f"x1_{x}{s}") for s in range(2)] for x in ("w_got", "x_got", "stored"))
        with nc.Block() as block:
            @block.sync
            def _(sp):
                def load(e, s):
                    xe = g.xbuf.rearrange("(e r) d -> e r d", r=CAP)[bass.ds(e, 1)].rearrange("o r d -> (o r) d")
                    sp.dma_start(xb[:, s, 0:RT - 1, :], xe[0:CAP - LR].rearrange("(t p) d -> p t d", p=P)).then_inc(x_got[s], 16)
                    sp.dma_start(xb[0:LR, s, RT - 1, :], xe[CAP - LR:CAP]).then_inc(x_got[s], 16)
                    sp.dma_start(w1[:, s], g.w1x1[bass.ds(e, 1)].rearrange("o p k f -> (o p) k f")).then_inc(w_got[s], 16)
                    sp.dma_start(b1[:, s], g.b1x1[bass.ds(e, 1)].rearrange("o p k -> (o p) k")).then_inc(w_got[s], 16)
                    sp.dma_start(w2[:, s], g.w2x1[bass.ds(e, 1)].rearrange("o p k f -> (o p) k f")).then_inc(w_got[s], 16)

                def store(e, s):
                    sp.wait_ge(y_taken, e * RT + (RT + 2))
                    ye = g.ybuf.rearrange("(e r) d -> e r d", r=CAP)[bass.ds(e, 1)].rearrange("o r d -> (o r) d")
                    sp.dma_start(ye[0:CAP - LR].rearrange("(t p) d -> p t d", p=P), yb[:, s, 0:RT - 1, :]).then_inc(stored[s], 16)
                    sp.dma_start(ye[CAP - LR:CAP], yb[0:LR, s, RT - 1, :]).then_inc(stored[s], 16)

                load(0, 0)
                load(1, 1)
                sp.dma_start(b2[:, :, :], g.b2x1.to_broadcast([P, XP, D])).then_inc(b2_got, 16)
                with sp.Fori(0, XP // 2 - 1) as i:
                    for s in range(2):
                        e = i * 2 + s
                        store(e, s)
                        sp.wait_ge(w_free, e + 2)
                        load(e + 2, s)
                        sp.wait_ge(stored[s], i * 32 + 32)
                        sp.sem_inc(y_free, 1)
                store(XP - 2, 0)
                store(XP - 1, 1)
                for s in range(2):
                    sp.wait_ge(stored[s], 32 * (XP // 2))

            @block.tensor
            def _(pe):
                pe.sem_inc(taken, 4)
                pe.sem_inc(y_taken, 2)
                pe.sem_inc(w_free, 1)
                pe.sem_inc(rows_free, 1)

                def turn_rows(e, s, uses):
                    pe.wait_ge(x_got[s], uses * 32)
                    pe.wait_ge(rows_free, e + 1)
                    for k in range(DB):
                        for t in range(RT):
                            n = P if t < RT - 1 else LR
                            last = pe.transpose(g.ps[k][:, t * P:t * P + n], xb[0:n, s, t, k * P:(k + 1) * P],
                                                g.ident[0:n, 0:n])
                    last.then_inc(turned, 1)

                def hidden(e, s, uses):
                    pe.wait_ge(w_got[s], uses * 48)
                    pe.wait_ge(xt_ready, e * 2 + 2)
                    pe.sem_inc(rows_free, 1)
                    for i in range(FB):
                        pe.wait_ge(taken, e * FB + (i + 1))
                        for k in range(DB):
                            last = pe.matmul(g.ps[2 + i % 4][:, 0:CAP], w1[:, s, k, i * P:(i + 1) * P], xt[:, s, k, :],
                                             start=k == 0, stop=k == DB - 1)
                        last.then_inc(formed, 1)

                def outputs(e, s):
                    pe.wait_ge(taken, e * FB + (FB + 4))
                    for t in range(RT):
                        n = P if t < RT - 1 else LR
                        pe.wait_ge(y_taken, e * RT + (t + 1))
                        for i in range(FB):
                            last = pe.matmul(g.ps[6 + t % 2][0:n, 0:D], ht[:, i, t * P:t * P + n], w2[:, s, i, :],
                                             start=i == 0, stop=i == FB - 1)
                        last.then_inc(y_formed, 1)
                    pe.wait_ge(y_formed, e * RT + RT)
                    pe.sem_inc(w_free, 1)

                turn_rows(0, 0, 1)
                with pe.Fori(0, XP // 2 - 1) as i:
                    for s in range(2):
                        e = i * 2 + s
                        hidden(e, s, i + 1)
                        turn_rows(e + 1, 1 - s, i + (1 + s))
                        outputs(e, s)
                hidden(XP - 2, 0, XP // 2)
                turn_rows(XP - 1, 1, XP // 2)
                outputs(XP - 2, 0)
                hidden(XP - 1, 1, XP // 2)
                outputs(XP - 1, 1)

            @block.scalar
            def _(act):
                def take_rows(e, s):
                    act.wait_ge(turned, e + 1)
                    act.copy(xt[:, s, 1, :], g.ps[1][:, 0:CAP]).then_inc(xt_ready, 1)

                def take(e, s):
                    for i in range(FB):
                        act.wait_ge(formed, e * FB + (i + 1))
                        act.activation(ht[:, i, :], g.ps[2 + i % 4][:, 0:CAP], ACT.Relu,
                                       bias=b1[:, s, i:i + 1]).then_inc(taken, 1)

                take_rows(0, 0)
                with act.Fori(0, XP // 2 - 1) as i:
                    for s in range(2):
                        e = i * 2 + s
                        act.wait_ge(w_free, e + 1)
                        take(e, s)
                        take_rows(e + 1, 1 - s)
                act.wait_ge(w_free, XP - 1)
                take(XP - 2, 0)
                take_rows(XP - 1, 1)
                act.wait_ge(w_free, XP)
                take(XP - 1, 1)

            @block.vector
            def _(v):
                def take_rows(e, s):
                    v.wait_ge(turned, e + 1)
                    v.tensor_copy(xt[:, s, 0, :], g.ps[0][:, 0:CAP]).then_inc(xt_ready, 1)

                def take(e, s):
                    v.wait_ge(y_free, e + 1)
                    for t in range(RT):
                        n = P if t < RT - 1 else LR
                        v.wait_ge(y_formed, e * RT + (t + 1))
                        v.tensor_tensor(yb[0:n, s, t, :], g.ps[6 + t % 2][0:n, 0:D],
                                        b2[0:n, bass.ds(e, 1), :].rearrange("p o d -> p (o d)"), ALU.add).then_inc(y_taken, 1)

                v.sem_inc(y_free, 2)
                take_rows(0, 0)
                v.wait_ge(b2_got, 16)
                with v.Fori(0, XP // 2 - 1) as i:
                    for s in range(2):
                        e = i * 2 + s
                        take_rows(e + 1, 1 - s)
                        take(e, s)
                take_rows(XP - 1, 1)
                take(XP - 2, 0)
                take(XP - 1, 1)


def finish(nc, g):
    K = 5
    BIG = 3.4028234663852886e38
    with ExitStack() as ctx:
        sb, sem = alloc(nc, ctx)
        y = sb("fi_y", [TN, NT, D])
        up, down = sb("fi_up", [TN, K, D]), sb("fi_down", [TN, K, D])
        got = [sem(f"fi_got{c}") for c in range(NT // K)]
        own, ready, stored = sem("fi_own"), sem("fi_ready"), sem("fi_stored")
        with nc.Block() as block:
            @block.gpsimd
            def _(pool):
                for j in range(NT):
                    pool.indirect_dma_start(y[:, j, :], None, g.ybuf, bass.IndirectOffsetOnAxis(
                        ap=g.home[:, j:j + 1], axis=0)).then_inc(got[j // K], 16)

            @block.vector
            def _(v):
                st = Steps(v, own)

                def do(ins):
                    st(ins)
                    st.settle()

                for c in range(NT // K):
                    s = slice(K * c, K * c + K)
                    v.wait_ge(got[c], 16 * K)
                    t = y[:, s, :]
                    do(v.tensor_tensor(t, t, g.share[:, s].unsqueeze(2).to_broadcast([TN, K, D]), ALU.mult))
                    st(v.tensor_scalar(up[:, :, :], t, BIG, -BIG, ALU.is_gt, ALU.mult))
                    st(v.tensor_scalar(down[:, :, :], t, -BIG, BIG, ALU.is_lt, ALU.mult))
                    st.settle()
                    st(v.tensor_scalar(up[:, :, :], up[:, :, :], BIG, 1e4, ALU.add, ALU.max))
                    st(v.tensor_scalar(down[:, :, :], down[:, :, :], BIG, -1e4, ALU.subtract, ALU.min))
                    st.settle()
                    for k in range(K):
                        tk = y[:, K * c + k, :]
                        st(v.scalar_tensor_tensor(up[:, k, :], tk, 0.0, up[:, k, :], ALU.max, ALU.min))
                        st(v.scalar_tensor_tensor(down[:, k, :], tk, 0.0, down[:, k, :], ALU.min, ALU.max))
                    st.settle()
                    do(v.tensor_tensor(up[:, :, :], up[:, :, :], down[:, :, :], ALU.add))
                    do(v.tensor_tensor(g.X[:, s, :], g.X[:, s, :], up[:, :, :], ALU.add))
                    v.sem_inc(ready, 1)

            @block.sync
            def _(sp):
                o = g.out.rearrange("(j p) d -> p j d", p=TN)
                for c in range(NT // K):
                    sp.wait_ge(ready, c + 1)
                    sp.dma_start(o[:, K * c:K * c + K, :], g.X[:, K * c:K * c + K, :]).then_inc(stored, 16)
                sp.wait_ge(stored, 16 * (NT // K))


def program(nc, out, **ins):
    g = Shared()
    (g.x, g.src, g.dst, g.edge_attr_128, g.w3t, g.w1_0, g.w2_0, g.cols0, g.rows0) = (
        ins[name] for name in ("x", "src", "dst", "edge_attr_128", "w3t", "w1_0", "w2_0", "cols0", "rows0"))
    (g.wkv0, g.wqt0, g.wout0, g.bout0, g.wr0, g.br0, g.w1x0, g.w2x0, g.b1x0) = (
        ins[name] for name in ("wkv0", "wqt0", "wout0", "bout0", "wr0", "br0", "w1x0", "w2x0", "b1x0"))
    (g.b2x0, g.gb0, g.w1h, g.a1h, g.wkv1, g.wqt1, g.wproj, g.bproj, g.wg1) = (
        ins[name] for name in ("b2x0", "gb0", "w1h", "a1h", "wkv1", "wqt1", "wproj", "bproj", "wg1"))
    (g.bg1, g.wg2, g.gcols1, g.gatew, g.gateb, g.w1x1, g.w2x1, g.b1x1, g.b2x1) = (
        ins[name] for name in ("bg1", "wg2", "gcols1", "gatew", "gateb", "w1x1", "w2x1", "b1x1", "b2x1"))
    g.out = out

    def dram(name, shape, dt=F32):
        return nc.dram_tensor(name, shape, dt, kind="Internal").ap()

    g.sorted = dram("sorted", (SLOTS, ROW))
    g.xbuf = dram("xbuf", (XP * CAP, D))
    g.ybuf = dram("ybuf", (XP * CAP, D))
    g.xnd = dram("xnd", (N, XROW))
    g.pvd = dram("pvd", (N, 4))
    g.hd = dram("hd", (N, HROW))
    with ExitStack() as ctx:
        sb, sem = alloc(nc, ctx)
        g.psum = ctx.enter_context(nc.psum_tensor("psum", [P, 8, 512], F32))
        g.ps = [g.psum[:, i, :] for i in range(8)]
        g.ident, g.before, g.after, g.ones, g.iota = (sb(x, [P, P]) for x in ("ident", "before", "after", "ones", "iota"))
        g.heads = sb("heads", [P, P])
        g.part = sb("part", [P, 1])
        g.XN = sb("XN", [TN, NT, XROW])
        g.deg, g.base = sb("deg", [TN, NT]), sb("base", [P, NT])
        g.gji, g.gfirst = sb("gji", [1, NG], I32), sb("gfirst", [P, NG])
        g.G, g.Q, g.WC = sb("G", [P, 2, DB, D]), sb("Q", [P, 2, D]), sb("WC", [P, DB, D])
        g.A8, g.ge = sb("A8", [P, DB, 8]), sb("ge", [P, 2, DE])
        g.bc, g.c8 = sb("bc", [1, D]), sb("c8", [1, 8])
        g.tabu = sb("tabu", [TN, 4, NT])
        g.sw, g.sdst = sb("sw", [P, 5, ST]), sb("sdst", [P, ST], I32)
        with ExitStack() as inner:
            g.X = alloc(nc, inner)[0]("X1", [TN, NT, D])
            setup(nc, g)
            g.XNT = alloc(nc, inner)[0]("XNT0", [P, DB, N])
            layer_norm(nc, g, g.X, g.XN[:, :, 0:D], "n0", g.XNT)
            gnn0_weights(nc, g)
            node_scores(nc, g)
        with ExitStack() as inner:
            own, _ = alloc(nc, inner)
            g.sl = own("sl", [P, 2, ET])
            g.srcf, g.lo = g.sl[:, 0, :], g.sl[:, 1, :]
            g.dsti, g.slot = own("dsti", [P, ET], I32), own("slot", [P, ET], I32)
            g.dstf, g.hi = (own(x, [P, ET]) for x in ("dstf", "hi"))
            g.found, g.pv = own("found", [P, ET, 5]), own("pv", [P, ET, 4])
            with ExitStack() as inner2:
                own2, _ = alloc(nc, inner2)
                g.hist = own2("hist", [TN, NT, ET])
                digits(nc, g)
                histogram(nc, g)
                with ExitStack() as inner3:
                    g.place = alloc(nc, inner3)[0]("place", [TN, NT, ET])
                    places(nc, g)
                locate(nc, g)
            scatter(nc, g)
        edge_weights(nc, g)
        g.mix = sb("mix", [P, DB, D])
        with ExitStack() as inner:
            g.XNT = alloc(nc, inner)[0]("XNT1", [P, DB, N])
            turn(nc, g, g.XN, g.XNT, "t1")
            key_softmax_context(nc, g, Context(g.wkv0, g.wqt0, g.wout0, float(32.0 ** 0.5)), 1, "kc0")
        g.X = None
        with ExitStack() as inner:
            g.acc = alloc(nc, inner)[0]("acc", [TN, NT, 2, D + 1 + DE + 1])
            gather_sums0(nc, g)
            g.X = alloc(nc, inner)[0]("X2", [TN, NT, D])
            g.XNT = alloc(nc, inner)[0]("XNT2", [P, DB, N])
            turn(nc, g, g.XN, g.XNT, "t2")
            combine0(nc, g)
            g.xsave = dram("xsave", (TN, NT, D))
            move(nc, g, g.xsave, g.X[:, :, :], "mv0")
        with ExitStack() as inner:
            sb, _ = alloc(nc, inner)
            g.X = sb("X3", [TN, NT, D])
            move(nc, g, g.X[:, :, :], g.xsave, "mv1")
            g.XNT = sb("XNT3", [P, DB, N])
            layer_norm(nc, g, g.X, g.XN[:, :, 0:D], "n1", g.XNT)
            with ExitStack() as inner2:
                sb2, _ = alloc(nc, inner2)
                g.w1e, g.w2e = sb2("w1e", [P, 2, DB, F0]), sb2("w2e", [P, 2, F0 // P, D])
                g.b1e, g.b2e = sb2("b1e", [P, 2, F0 // P]), sb2("b2e", [1, D])
                route0(nc, g)
                experts0(nc, g)
            layer_norm(nc, g, g.XN[:, :, 0:D], g.XN[:, :, 0:D], "n2")
            scaled_residual(nc, g)
            layer_norm(nc, g, g.X, g.XN[:, :, 0:D], "n3", g.XNT)
            with ExitStack() as inner2:
                sb2, _ = alloc(nc, inner2)
                g.H = sb2("H", [TN, NT, HROW])
                g.acc1 = sb2("acc1", [TN, NT, D + 4])
                hidden1(nc, g)
                gather_sums1(nc, g)
                combine1(nc, g)
            key_softmax_context(nc, g, Context(g.wkv1, g.wqt1, None, 1.0), 2, "kc1")
            with ExitStack() as inner2:
                sb2, _ = alloc(nc, inner2)
                g.XGT = sb2("XGT", [P, DB, N])
                g.wg1t, g.wg2t, g.wprojt = sb2("wg1t", [P, DB, D // 4]), sb2("wg2t", [D // 4, D]), sb2("wprojt", [P, DB, D])
                g.gcols, g.bg1t, g.bprojt = sb2("gcols", [P, 6]), sb2("bg1t", [D // 4, 1]), sb2("bprojt", [1, D])
                gate_weights(nc, g)
                layer_norm(nc, g, g.XN[:, :, 0:D], g.XN[:, :, 0:D], "n4", g.XGT, g.gcols[:, 0:2], g.gcols[:, 2:4])
                gated_mix(nc, g)
            layer_norm(nc, g, g.X, g.XN[:, :, 0:D], "n5", g.XNT)
            g.share, g.home = sb("share", [TN, NT]), sb("home", [TN, NT], I32)
            route1(nc, g)
            experts1(nc, g)
            finish(nc, g)


def layout(I):
    import numpy as np

    def cols(a, n):
        a = a.reshape(a.shape[:-1] + (n, P))
        return np.moveaxis(a, -1, 0)

    o = {k: I[k] for k in ("x", "src", "dst", "edge_attr_128")}
    o["w3t"] = I["L0_gnn_W3w"].reshape(2, D, 5, P).transpose(3, 0, 2, 1)
    o["w1_0"] = I["L0_gnn_W1w"].reshape(2, DB, P, D).transpose(2, 0, 1, 3)
    o["w2_0"] = I["L0_gnn_W2w"].transpose(1, 0, 2)
    av = np.stack([I["L0_gnn_aVw"][:, 0, 0:D], I["L0_gnn_aVw"][:, 0, D:], I["L0_gnn_aEw"][:, 0, 0:D],
                   I["L0_gnn_aEw"][:, 0, D:2 * D]], 1)
    av = cols(av, DB).transpose(0, 1, 3, 2).reshape(P, 16)
    o["cols0"] = np.concatenate([av, I["L0_gnn_aEw"][:, 0, 2 * D:].T, cols(I["L0_gnn_W1b"], DB).reshape(P, 4),
                                 I["L0_gnn_W2b"].T], 1)
    o["rows0"] = np.concatenate([I["L0_gnn_W3b"].reshape(-1), I["L0_gnn_aVb"].reshape(-1),
                                 I["L0_gnn_aEb"].reshape(-1)])[None]
    w = I["L0_mix_W_qkv"].reshape(DB, P, 3, P)
    o["wkv0"] = w[:, :, 1:].transpose(1, 0, 2, 3).reshape(P, DB, 2 * P)
    o["wqt0"] = w[:, :, 0].reshape(D, P).T[:, None, :]
    o["wout0"], o["bout0"] = I["L0_mix_W_out"], I["L0_mix_b_out"][None]
    o["wr0"], o["br0"] = I["L0_ffn_Wr"].reshape(DB, P, XP).transpose(1, 0, 2), I["L0_ffn_br"][None]
    o["w1x0"] = I["L0_ffn_W1"].reshape(XP, DB, P, F0).transpose(0, 2, 1, 3)
    o["w2x0"] = I["L0_ffn_W2"].reshape(XP, F0 // P, P, D).transpose(0, 2, 1, 3)
    o["b1x0"], o["b2x0"] = I["L0_ffn_b1"].reshape(XP, F0 // P, P).transpose(0, 2, 1), I["L0_ffn_b2"]
    o["gb0"] = np.stack([I["L0_ffn_gamma"], I["L0_ffn_beta"]])[None]
    o["w1h"] = I["L1_gnn_W"].reshape(4, DB, P, D // 4).transpose(2, 1, 0, 3).reshape(P, DB, D)
    a = I["L1_gnn_a"].reshape(4, 2, D // 4)
    o["a1h"] = np.stack([a[:, 1].reshape(-1), a[:, 0].reshape(-1)])[None]
    w = I["L1_mix_Wqkv"]
    o["wkv1"] = w[:, D:].reshape(DB, P, 2 * D).transpose(1, 0, 2)
    o["wqt1"] = w[:, 0:D].T.reshape(DB, P, D).transpose(1, 0, 2)
    o["wproj"], o["bproj"] = I["L1_mix_Wproj"].reshape(DB, P, D).transpose(1, 0, 2), I["L1_mix_bproj"][None]
    o["wg1"], o["bg1"] = I["L1_mix_Wg1"].reshape(DB, P, D // 4).transpose(1, 0, 2), I["L1_mix_bg1"][:, None]
    o["wg2"] = I["L1_mix_Wg2"]
    o["gcols1"] = np.concatenate([cols(I[k], DB) for k in ("L1_mix_ln_g", "L1_mix_ln_b", "L1_mix_bg2")], 1)
    o["gatew"], o["gateb"] = I["L1_ffn_gate_w"].reshape(DB, P, XP).transpose(1, 0, 2), I["L1_ffn_gate_b"][None]
    o["w1x1"] = I["L1_ffn_w1"].reshape(XP, DB, P, F1).transpose(0, 2, 1, 3)
    o["w2x1"] = I["L1_ffn_w2"].reshape(XP, F1 // P, P, D).transpose(0, 2, 1, 3)
    o["b1x1"], o["b2x1"] = I["L1_ffn_b1"].reshape(XP, F1 // P, P).transpose(0, 2, 1), I["L1_ffn_b2"][None]
    return {k: np.ascontiguousarray(v) for k, v in o.items()}


def kernel(**inputs):
    import numpy as np
    import concourse.bacc as bacc
    from concourse.bass_utils import run_bass_kernel_spmd

    nc = bacc.Bacc("TRN2", target_bir_lowering=False, num_devices=1)
    arrays = {f"in_{name}": a for name, a in layout({k: np.asarray(v) for k, v in inputs.items()}).items()}
    args = {name[3:]: nc.dram_tensor(name, a.shape, mybir.dt.from_np(a.dtype), kind="ExternalInput").ap()
            for name, a in arrays.items()}
    out = nc.dram_tensor("out", (N, D), F32, kind="ExternalOutput").ap()
    program(nc, out, **args)
    return run_bass_kernel_spmd(nc, [arrays], core_ids=[0]).results[0]["out"]
```
